# Optimizing a Trainium2 kernel written in Bass

```python
import numpy as np
import jax
import jax.numpy as jnp

def _softmax(x, axis=-1):
    return jax.nn.softmax(x, axis=axis)

def _gelu(x):
    return jax.nn.gelu(x, approximate=True)

def _silu(x):
    return jax.nn.silu(x)

def _sigmoid(x):
    return jax.nn.sigmoid(x)

def _layernorm(x, axis=-1, eps=1e-05):
    m = jnp.mean(x, axis=axis, keepdims=True)
    v = jnp.var(x, axis=axis, keepdims=True)
    return (x - m) / jnp.sqrt(v + eps)

def _scatter_add(tgt, idx, src, axis=0):
    return tgt.at[idx].add(src)

def _segment_sum(src, seg, n):
    return jax.ops.segment_sum(src, seg, n)
kernel_name = 'mk_recurrent_d2_jaxref_r4_4bff7c'

def setup_inputs(seed: int=0):
    np.random.seed(seed)
    _w = jnp.asarray

    def _L0_attn_setup():
        import jax, jax.numpy as jnp
        import numpy as np
        D = 256
        HEADS = 16
        LN_EPS = 1e-05
        SHEP_EPS = 0.0001
        SHEP_P = 2

        def _shepards_mha(Q, K, V):
            q2 = jnp.sum(Q * Q, axis=-1, keepdims=True)
            k2 = jnp.sum(K * K, axis=-1, keepdims=True)
            sq = q2 + jnp.swapaxes(k2, -1, -2) - 2.0 * jnp.einsum('bhqd,bhkd->bhqk', Q, K)
            dist = jnp.sqrt(jnp.maximum(sq, 0.0))
            W = (SHEP_EPS + dist) ** (-SHEP_P)
            W = W / (SHEP_EPS + jnp.sum(W, axis=-1, keepdims=True))
            return jnp.einsum('bhqk,bhkd->bhqd', W, V)
        key = jax.random.key(seed)
        k1, k2, k3 = jax.random.split(key, 3)
        b, t, d = (2, 512, D)
        X = jax.random.normal(k1, (b, t, d), dtype=jnp.float32)
        W_in = jax.random.normal(k2, (4 * d, d), dtype=jnp.float32) * (1.0 / np.sqrt(d))
        b_in = jnp.zeros((4 * d,), dtype=jnp.float32)
        W_out = jax.random.normal(k3, (d, d), dtype=jnp.float32) * (1.0 / np.sqrt(d))
        b_out = jnp.zeros((d,), dtype=jnp.float32)
        return {'X': X, 'W_in': W_in, 'b_in': b_in, 'W_out': W_out, 'b_out': b_out}
    _L0_attn_in = _L0_attn_setup()

    def _L0_ffn_setup():
        import jax, jax.numpy as jnp
        import numpy as np

        def _bitlinear(x, w_latent):
            scale = jax.lax.stop_gradient(jnp.clip(jnp.mean(jnp.abs(w_latent), axis=1, keepdims=True), 1e-05, None))
            tern = jnp.clip(jnp.round(w_latent / scale), -1.0, 1.0)
            w = w_latent + jax.lax.stop_gradient(tern - w_latent)
            return x @ (w * scale).T
        key = jax.random.key(seed)
        ks = jax.random.split(key, 6)
        dim, hidden, rank = (256, 1024, 16)
        B, S = (4, 1024)
        x = jax.random.normal(ks[0], (B, S, dim), dtype=jnp.float32)
        w_fc = 0.02 * jax.random.normal(ks[1], (hidden, dim), dtype=jnp.float32)
        w_proj = 0.02 * jax.random.normal(ks[2], (dim, hidden), dtype=jnp.float32)
        u = 0.02 * jax.random.normal(ks[3], (hidden, rank), dtype=jnp.float32)
        v = 0.02 * jax.random.normal(ks[4], (rank, dim), dtype=jnp.float32)
        fast_b = jax.random.normal(ks[5], (rank, rank), dtype=jnp.float32)
        gate = jnp.float32(0.05)
        return {'x': x, 'fast_b': fast_b, 'w_fc': w_fc, 'w_proj': w_proj, 'u': u, 'v': v, 'gate': gate}
    _L0_ffn_in = _L0_ffn_setup()

    def _L1_attn_setup():
        import jax, jax.numpy as jnp
        import numpy as np
        D_IN = 256
        D_OUT = 256
        NUM_HEADS = 16
        HEAD_DIM = D_OUT // NUM_HEADS
        EPS = 1e-06
        POW = 16.0

        def _l2norm(t):
            n = jnp.sqrt(jnp.sum(t * t, axis=-1, keepdims=True))
            return t / jnp.maximum(n, EPS)
        key = jax.random.key(seed)
        ks = jax.random.split(key, 6)
        s = 1.0 / np.sqrt(D_IN)
        x = jax.random.normal(ks[0], (2, 512, D_IN), dtype=jnp.float32)
        Wq = jax.random.uniform(ks[1], (D_OUT, D_IN), jnp.float32, -s, s)
        Wk = jax.random.uniform(ks[2], (D_OUT, D_IN), jnp.float32, -s, s)
        Wv = jax.random.uniform(ks[3], (D_OUT, D_IN), jnp.float32, -s, s)
        Wo = jax.random.uniform(ks[4], (D_OUT, D_OUT), jnp.float32, -s, s)
        bo = jax.random.uniform(ks[5], (D_OUT,), jnp.float32, -s, s)
        return {'x': x, 'Wq': Wq, 'Wk': Wk, 'Wv': Wv, 'Wo': Wo, 'bo': bo}
    _L1_attn_in = _L1_attn_setup()

    def _L1_ffn_setup():
        import jax, jax.numpy as jnp
        import numpy as np
        EPS = 1e-05

        def _quantize(W):
            gamma = jnp.mean(jnp.abs(W))
            return jnp.clip(jnp.round(W / (gamma + EPS)), -1.0, 1.0)
        key = jax.random.key(seed)
        k_x, k_w1, k_b1, k_w2, k_b2 = jax.random.split(key, 5)
        n_embd = 256
        d_ff = 4 * n_embd
        B, S = (4, 1024)
        bound1 = 1.0 / np.sqrt(n_embd)
        bound2 = 1.0 / np.sqrt(d_ff)
        x = jax.random.normal(k_x, (B, S, n_embd), dtype=jnp.float32)
        W1 = jax.random.uniform(k_w1, (d_ff, n_embd), jnp.float32, -bound1, bound1)
        b1 = jax.random.uniform(k_b1, (d_ff,), jnp.float32, -bound1, bound1)
        W2 = jax.random.uniform(k_w2, (n_embd, d_ff), jnp.float32, -bound2, bound2)
        b2 = jax.random.uniform(k_b2, (n_embd,), jnp.float32, -bound2, bound2)
        return {'x': x, 'W1': W1, 'b1': b1, 'W2': W2, 'b2': b2}
    _L1_ffn_in = _L1_ffn_setup()
    _d = {'L0_attn_X': _L0_attn_in['X'], 'L0_attn_W_in': _L0_attn_in['W_in'], 'L0_attn_b_in': _L0_attn_in['b_in'], 'L0_attn_W_out': _L0_attn_in['W_out'], 'L0_attn_b_out': _L0_attn_in['b_out'], 'L0_ffn_fast_b': _L0_ffn_in['fast_b'], 'L0_ffn_w_fc': _L0_ffn_in['w_fc'], 'L0_ffn_w_proj': _L0_ffn_in['w_proj'], 'L0_ffn_u': _L0_ffn_in['u'], 'L0_ffn_v': _L0_ffn_in['v'], 'L0_ffn_gate': _L0_ffn_in['gate'], 'L1_attn_Wq': _L1_attn_in['Wq'], 'L1_attn_Wk': _L1_attn_in['Wk'], 'L1_attn_Wv': _L1_attn_in['Wv'], 'L1_attn_Wo': _L1_attn_in['Wo'], 'L1_attn_bo': _L1_attn_in['bo'], 'L1_ffn_W1': _L1_ffn_in['W1'], 'L1_ffn_b1': _L1_ffn_in['b1'], 'L1_ffn_W2': _L1_ffn_in['W2'], 'L1_ffn_b2': _L1_ffn_in['b2']}
    _x0 = _d['L0_attn_X']
    _d['L0_attn_X'] = jax.random.normal(jax.random.fold_in(jax.random.key(seed), 1), (2, 2048, 256), dtype=_x0.dtype)
    del _x0
    return _d

def reference(L0_attn_X, L0_attn_W_in, L0_attn_b_in, L0_attn_W_out, L0_attn_b_out, L0_ffn_fast_b, L0_ffn_w_fc, L0_ffn_w_proj, L0_ffn_u, L0_ffn_v, L0_ffn_gate, L1_attn_Wq, L1_attn_Wk, L1_attn_Wv, L1_attn_Wo, L1_attn_bo, L1_ffn_W1, L1_ffn_b1, L1_ffn_W2, L1_ffn_b2):

    def _L0_attn_ref(X, W_in, b_in, W_out, b_out):
        import jax, jax.numpy as jnp
        import numpy as np
        D = 256
        HEADS = 16
        LN_EPS = 1e-05
        SHEP_EPS = 0.0001
        SHEP_P = 2

        def _shepards_mha(Q, K, V):
            q2 = jnp.sum(Q * Q, axis=-1, keepdims=True)
            k2 = jnp.sum(K * K, axis=-1, keepdims=True)
            sq = q2 + jnp.swapaxes(k2, -1, -2) - 2.0 * jnp.einsum('bhqd,bhkd->bhqk', Q, K)
            dist = jnp.sqrt(jnp.maximum(sq, 0.0))
            W = (SHEP_EPS + dist) ** (-SHEP_P)
            W = W / (SHEP_EPS + jnp.sum(W, axis=-1, keepdims=True))
            return jnp.einsum('bhqk,bhkd->bhqd', W, V)
        b, t, d = X.shape
        h = HEADS
        dh = d // h
        mu = jnp.mean(X, axis=-1, keepdims=True)
        var = jnp.mean((X - mu) ** 2, axis=-1, keepdims=True)
        Xn = (X - mu) / jnp.sqrt(var + LN_EPS)
        P = jnp.einsum('btd,ed->bte', Xn, W_in) + b_in
        P = P.reshape(b, t, h, 4 * dh).transpose(0, 2, 1, 3)
        Q, K, V, G = jnp.split(P, 4, axis=-1)
        A = _shepards_mha(Q, K, V)
        O = (G * A).transpose(0, 2, 1, 3).reshape(b, t, d)
        return X + jnp.einsum('btd,ed->bte', O, W_out) + b_out

    def _L0_ffn_ref(x, fast_b, w_fc, w_proj, u, v, gate):
        import jax, jax.numpy as jnp
        import numpy as np

        def _bitlinear(x, w_latent):
            scale = jax.lax.stop_gradient(jnp.clip(jnp.mean(jnp.abs(w_latent), axis=1, keepdims=True), 1e-05, None))
            tern = jnp.clip(jnp.round(w_latent / scale), -1.0, 1.0)
            w = w_latent + jax.lax.stop_gradient(tern - w_latent)
            return x @ (w * scale).T
        h = _bitlinear(x, w_fc) + gate * (x @ v.T @ fast_b.T @ u.T)
        r = jnp.maximum(h, 0.0)
        return _bitlinear(r * r, w_proj)

    def _L1_attn_ref(x, Wq, Wk, Wv, Wo, bo):
        import jax, jax.numpy as jnp
        import numpy as np
        D_IN = 256
        D_OUT = 256
        NUM_HEADS = 16
        HEAD_DIM = D_OUT // NUM_HEADS
        EPS = 1e-06
        POW = 16.0

        def _l2norm(t):
            n = jnp.sqrt(jnp.sum(t * t, axis=-1, keepdims=True))
            return t / jnp.maximum(n, EPS)
        B, T, _ = x.shape

        def heads(W):
            y = jnp.einsum('btd,od->bto', x, W)
            return y.reshape(B, T, NUM_HEADS, HEAD_DIM).transpose(0, 2, 1, 3)
        Q = _l2norm(heads(Wq))
        K = _l2norm(heads(Wk))
        V = heads(Wv)
        cos_sim = jnp.clip(jnp.einsum('bhtd,bhsd->bhts', Q, K), -0.999, 0.999)
        scores = 1.0 - jnp.arccos(cos_sim) / jnp.pi
        W = jnp.power(jnp.maximum(scores, EPS), POW)
        W = W / (jnp.sum(W, axis=-1, keepdims=True) + EPS)
        out = jnp.einsum('bhts,bhsd->bhtd', W, V)
        out = out.transpose(0, 2, 1, 3).reshape(B, T, D_OUT)
        return jnp.einsum('bto,po->btp', out, Wo) + bo

    def _L1_ffn_ref(x, W1, b1, W2, b2):
        import jax, jax.numpy as jnp
        import numpy as np
        EPS = 1e-05

        def _quantize(W):
            gamma = jnp.mean(jnp.abs(W))
            return jnp.clip(jnp.round(W / (gamma + EPS)), -1.0, 1.0)
        Wq1 = _quantize(W1)
        Wq2 = _quantize(W2)
        h = jax.nn.relu(jnp.einsum('bsd,fd->bsf', x, Wq1) + b1)
        out = jnp.einsum('bsf,df->bsd', h, Wq2) + b2
        return out
    x = L0_attn_X
    xn = _layernorm(x, axis=-1)
    s = _L0_attn_ref(xn, L0_attn_W_in, L0_attn_b_in, L0_attn_W_out, L0_attn_b_out)
    g = _silu(_L0_ffn_ref(xn, L0_ffn_fast_b, L0_ffn_w_fc, L0_ffn_w_proj, L0_ffn_u, L0_ffn_v, L0_ffn_gate))
    x = x + s * g
    xn = _layernorm(x, axis=-1)
    s = _L1_attn_ref(xn, L1_attn_Wq, L1_attn_Wk, L1_attn_Wv, L1_attn_Wo, L1_attn_bo)
    g = _silu(_L1_ffn_ref(xn, L1_ffn_W1, L1_ffn_b1, L1_ffn_W2, L1_ffn_b2))
    x = x + s * g
    return x

_drawn_inputs = setup_inputs


def setup_inputs(seed=0):
    import zlib

    import numpy as np

    out = dict(_drawn_inputs(seed))
    spreads = {'L0_attn_b_in': (0.0, 0.8), 'L0_attn_b_out': (0.0, 2.0)}
    factors = {'L0_attn_W_in': 8.0,
     'L0_attn_W_out': 8.0,
     'L0_ffn_fast_b': 8.0,
     'L0_ffn_u': 8.0,
     'L0_ffn_v': 8.0,
     'L1_ffn_b1': 200.0,
     'L1_ffn_b2': 200.0}
    for name, (base, spread) in spreads.items():
        noise = np.random.default_rng([zlib.crc32(name.encode()), seed]).standard_normal(out[name].shape)
        drawn = base * np.exp(spread * noise) if base else spread * noise
        out[name] = jnp.asarray(drawn.astype(out[name].dtype))
    for name, factor in factors.items():
        out[name] = (out[name] * factor).astype(out[name].dtype)
    return out
```

```python
import concourse.bass as bass
from concourse import mybir
from contextlib import ExitStack

F32 = mybir.dt.float32
BF16 = mybir.dt.bfloat16
ALU = mybir.AluOpType
ACT = mybir.ActivationFunctionType
X = mybir.AxisListType.X

B, T, D = 2, 2048, 256
HEADS = 16
DH = D // HEADS
HID = 4 * D
RANK = 16
P = 128
NT = B * T // P
KT = T // P
KD = D // P
FT = HID // P
QB = T // 512
TB = B * T // 512
NQK = 2 * D // P
VW = 32
LN_EPS = 1e-5
SHEP_EPS = 1e-4
NORM_EPS = 1e-6
SUM_EPS1 = 1e-6
COS_MAX = 0.999
PI = 3.141592653589793

PRODUCTS = [(0, 0), (0, 1), (0, 2), (1, 0), (1, 1), (2, 0)]
ROWS = DH * len(PRODUCTS)
NORM_ROWS = 6


class Mem:

    def __init__(self, nc, ctx):
        def sb(name, shape, dt=F32):
            return ctx.enter_context(nc.sbuf_tensor(name, shape, dt))

        self.w1T = sb("w1T", [P, KD, HID])
        self.w2T = sb("w2T", [P, FT, D])
        self.values = sb("values", [P, NT, D])
        self.gated = sb("gated", [P, NT, D])
        self.work = sb("work", [P, 3 * NT * D])
        self.q_stack = [sb(f"q_stack{b}", [P, T], BF16) for b in range(B)]
        self.k_stack = [sb(f"k_stack{b}", [P, T], BF16) for b in range(B)]
        self.v_tile = [sb(f"v_tile{b}", [P, KT, VW]) for b in range(B)]
        self.hidden = sb("hidden", [P, FT, P])
        self.ffn_in = sb("ffn_in", [P, KD, P])
        self.ffn_out = sb("ffn_out", [P, D])
        self.head_outT = sb("head_outT", [P, 512])
        self.ident = sb("ident", [P, P])
        self.ones_row = sb("ones_row", [1, P])
        self.b1_tiles = sb("b1_tiles", [FT, P])
        self.b2_row = sb("b2_row", [1, D])
        self.small = sb("small", [P, 8, NT])
        self.den = sb("den", [P, 2, KT])
        self.psS = [ctx.enter_context(nc.psum_tensor(f"psS{i}", [P, 1024], F32)) for i in range(2)]
        self.psO = [ctx.enter_context(nc.psum_tensor(f"psO{i}", [P, 512], F32)) for i in range(2)]
        self.psM = [ctx.enter_context(nc.psum_tensor(f"psM{i}", [P, 512], F32)) for i in range(2)]

    def area(self, start, *shape):
        n = 1
        for s in shape:
            n *= s
        flat = self.work[:, start:start + n]
        if len(shape) == 1:
            return flat
        names = "abc"[:len(shape)]
        return flat.rearrange(f"p ({' '.join(names)}) -> p {' '.join(names)}",
                              **{c: s for c, s in zip(names, shape)})


class Chain:

    def __init__(self, eng, sem):
        self.eng, self.sem, self.n = eng, sem, 0

    def __call__(self, ins):
        self.n += 1
        ins.then_inc(self.sem, 1)
        self.eng.wait_ge(self.sem, self.n)


def sems(nc, ctx, prefix, *names):
    made = [ctx.enter_context(nc.semaphore(f"{prefix}_{n}")) for n in names]
    ctx.callback(clear, nc, made)
    return made


def clear(nc, made):
    with nc.Block() as block:
        @block.sync
        def _(sp):
            for s in made:
                sp.sem_clear(s)


def constants_phase(nc, m, io):
    with ExitStack() as ctx:
        s_ident, s_set = sems(nc, ctx, "const", "ident", "set")
        block = ctx.enter_context(nc.Block())

        @block.sync
        def _(sp):
            sp.dma_start(m.ident[:, :], io["ident"]).then_inc(s_ident, 16)
            sp.wait_ge(s_ident, 16)

        @block.vector
        def _(dve):
            nc.vector.memset(m.ones_row[:, :], 1.0).then_inc(s_set, 1)
            for b in range(B):
                nc.vector.memset(m.v_tile[b][:, :, DH:DH + 1], 1.0).then_inc(s_set, 1)
                nc.vector.memset(m.v_tile[b][:, :, DH + 1:VW], 0.0).then_inc(s_set, 1)
                nc.vector.memset(m.q_stack[b][ROWS:P, :], 1.0).then_inc(s_set, 1)
                nc.vector.memset(m.k_stack[b][ROWS:P, :], 1.0).then_inc(s_set, 1)
            dve.wait_ge(s_set, 1 + 4 * B)


def weights_phase(nc, m, io, L):
    pre = f"w{L}"
    w1, w2 = (io["w_fc"], io["w_proj"]) if L == 0 else (io["W1"], io["W2"])
    BASE = NT * D
    raw1 = m.area(BASE, FT, D)
    raw2 = m.area(BASE + FT * D, KD, HID)
    mag = m.area(BASE + 2 * FT * D, FT, D)
    mag2 = m.area(BASE + 2 * FT * D, KD, HID)
    neg = m.area(BASE + 5 * FT * D, HID)
    u_T = m.area(BASE + 3 * FT * D + HID, HID)
    v_sb = m.area(BASE + 3 * FT * D + 2 * HID, D)
    fastT = m.area(BASE + 3 * FT * D + 2 * HID + D, RANK)
    gate = m.area(BASE + 3 * FT * D + 2 * HID + D + RANK, 1)
    gate_all = m.area(BASE + 3 * FT * D + 2 * HID + D + RANK + 1, 1)
    fv = m.area(BASE + 3 * FT * D + 2 * HID + 2 * D, D)
    ones = m.area(BASE + 3 * FT * D, P)
    S, HALF, NHALF = 0, 1, 2
    n_loads = 2 + (4 if L == 0 else 2)
    with ExitStack() as ctx:
        s_load, s_dve, s_sum, s_rows, s_tern, s_tr, s_out, s_g, s_ga, s_fv, s_fvc, s_lr, s_add = sems(
            nc, ctx, pre, "load", "dve", "rows", "total", "tern", "transposed", "copied", "gate", "gate_copied",
            "fv", "fv_copied", "lowrank", "added")
        block = ctx.enter_context(nc.Block())

        @block.sync
        def _(sp):
            sp.dma_start(raw1, w1.rearrange("(f p) i -> p f i", p=P)).then_inc(s_load, 16)
            sp.dma_start(raw2, w2.rearrange("(k p) j -> p k j", p=P)).then_inc(s_load, 16)
            if L == 0:
                sp.dma_start(u_T[0:RANK, :], io["u_T"]).then_inc(s_load, 16)
                sp.dma_start(v_sb[0:RANK, :], io["v"]).then_inc(s_load, 16)
                sp.dma_start(fastT[0:RANK, :], io["fast_bT"]).then_inc(s_load, 16)
                sp.dma_start(gate[0:1, :], io["gate"]).then_inc(s_load, 16)
            else:
                sp.dma_start(m.b1_tiles[:, :], io["b1"]).then_inc(s_load, 16)
                sp.dma_start(m.b2_row[:, :], io["b2"]).then_inc(s_load, 16)
            sp.wait_ge(s_load, 16 * n_loads)

        @block.vector
        def _(dve):
            link = Chain(dve, s_dve)
            if L == 1:
                link(nc.vector.memset(ones, 1.0))
            dve.wait_ge(s_load, 16 * n_loads)
            for i, (raw, mg, n, width) in enumerate(((raw1, mag, FT, D), (raw2, mag2, KD, HID))):
                c = slice(8 * i, 8 * i + n)
                link(nc.vector.scalar_tensor_tensor(mg, raw, -1.0, raw, ALU.mult, ALU.max))
                if L == 0:
                    link(nc.vector.tensor_reduce(m.small[:, S, c], mg, axis=X, op=ALU.add))
                    link(nc.vector.tensor_scalar(m.small[:, S, c], m.small[:, S, c], 1.0 / width, 1e-5,
                                                 ALU.mult, ALU.max))
                else:
                    nc.vector.tensor_reduce(m.small[:, 3, c], mg, axis=X, op=ALU.add).then_inc(s_sum, 1)
                    dve.wait_ge(s_rows, i + 1)
                    link(nc.vector.tensor_reduce(m.small[:, 4, i:i + 1], m.psM[i][:, 0:n], axis=X, op=ALU.add))
                    link(nc.vector.tensor_scalar(m.small[:, 5, i:i + 1], m.small[:, 4, i:i + 1],
                                                 1.0 / (D * HID), 1e-5, ALU.mult, ALU.add))
                    for j in range(n):
                        link(nc.vector.tensor_copy(m.small[:, S, 8 * i + j:8 * i + j + 1], m.small[:, 5, i:i + 1]))
                link(nc.vector.tensor_scalar(m.small[:, HALF, c], m.small[:, S, c], 0.5, None, ALU.mult))
                link(nc.vector.tensor_scalar(m.small[:, NHALF, c], m.small[:, S, c], -0.5, None, ALU.mult))
                for j in range(n):
                    a = slice(8 * i + j, 8 * i + j + 1)
                    link(nc.vector.tensor_scalar(neg[:, 0:width], raw[:, j, :], m.small[:, NHALF, a], None, ALU.is_lt))
                    link(nc.vector.scalar_tensor_tensor(raw[:, j, :], raw[:, j, :], m.small[:, HALF, a],
                                                        neg[:, 0:width], ALU.is_gt, ALU.subtract))
                    if L == 0:
                        link(nc.vector.tensor_scalar(raw[:, j, :], raw[:, j, :], m.small[:, S, a], None, ALU.mult))
            nc.vector.tensor_copy(m.small[:, 6, 0:1], m.small[:, S, 0:1]).then_inc(s_tern, 1)
            dve.wait_ge(s_tr, 1)
            for k in range(KD):
                nc.vector.tensor_copy(m.w1T[:, k, :], m.psS[k][:, :]).then_inc(s_out, 1)
            for j in range(4):
                ps = (m.psO + m.psM)[j]
                nc.vector.tensor_copy(m.w2T[:, 2 * j:2 * j + 2, :], ps[:, :].rearrange("p (a d) -> p a d", a=2))\
                    .then_inc(s_out, 1)
            if L == 0:
                dve.wait_ge(s_g, 1)
                nc.vector.tensor_copy(gate_all[0:RANK, :], m.psM[1][0:RANK, 0:1]).then_inc(s_ga, 1)
                dve.wait_ge(s_ga, 1)
                dve.wait_ge(s_fv, 1)
                nc.vector.tensor_scalar(fv[0:RANK, :], m.psM[0][0:RANK, 0:D], gate_all[0:RANK, :], None, ALU.mult)\
                    .then_inc(s_fvc, 1)
                for k in range(KD):
                    dve.wait_ge(s_lr, k + 1)
                    nc.vector.tensor_tensor(m.w1T[:, k, :], m.psS[k][:, :], m.w1T[:, k, :], ALU.add)\
                        .then_inc(s_add, 1)
                dve.wait_ge(s_add, KD)

        @block.tensor
        def _(pe):
            if L == 1:
                for i, n in enumerate((FT, KD)):
                    pe.wait_ge(s_sum, i + 1)
                    nc.tensor.matmul(m.psM[i][:, 0:n], ones, m.small[:, 3, 8 * i:8 * i + n],
                                     start=True, stop=True).then_inc(s_rows, 1)
            pe.wait_ge(s_tern, 1)
            for k in range(KD):
                for f in range(FT):
                    nc.tensor.transpose(m.psS[k][:, f * P:(f + 1) * P], raw1[:, f, k * P:(k + 1) * P], m.ident[:, :])
            for j in range(FT):
                ps = (m.psO + m.psM)[j // 2]
                for k in range(KD):
                    c = (j % 2) * D + k * P
                    last = nc.tensor.transpose(ps[:, c:c + P], raw2[:, k, j * P:(j + 1) * P], m.ident[:, :])
            last.then_inc(s_tr, 1)
            if L == 0:
                pe.wait_ge(s_out, 6)
                nc.tensor.matmul(m.psM[1][0:RANK, 0:1], m.ones_row[0:1, 0:RANK], gate[0:1, :], start=True, stop=True)\
                    .then_inc(s_g, 1)
                nc.tensor.matmul(m.psM[0][0:RANK, 0:D], fastT[0:RANK, :], v_sb[0:RANK, :], start=True, stop=True)\
                    .then_inc(s_fv, 1)
                pe.wait_ge(s_fvc, 1)
                for k in range(KD):
                    for c in range(2):
                        last = nc.tensor.matmul(m.psS[k][:, c * 512:(c + 1) * 512], fv[0:RANK, k * P:(k + 1) * P],
                                                u_T[0:RANK, c * 512:(c + 1) * 512], start=True, stop=True)
                    last.then_inc(s_lr, 1)


def norm_phase(nc, m, io, L):
    pre = f"n{L}"
    x_sb = m.area(0, NT, D)
    x2_sb = m.area(NT * D, NT, D)
    xTa = m.area(2 * NT * D, KD, B * T)
    xTf = m.values[:, :, :].rearrange("p a b -> p (a b)").rearrange("p (k t) -> p k t", k=KD)
    MEAN, VAR, RSTD, T0, T1 = 0, 1, 2, 3, 4
    CH = 4
    stats = m.hidden[:, 0:2, :].rearrange("p a b -> p (a b)")[:, 0:NT * 6].rearrange("p (t s) -> p t s", s=6)
    x_view = io["x"].rearrange("(t p) d -> p t d", p=P)
    norms = 2 if L == 0 else 1
    with ExitStack() as ctx:
        s_stat, s_dve, s_var, s_std, s_norm, s_tr, s_fr, s_fr2, s_st = sems(
            nc, ctx, pre, "stats", "dve", "var", "std", "normed", "transposed", "freed_by_act", "freed_by_dve",
            "stored")
        s_x = sems(nc, ctx, pre, *[f"x{c}" for c in range(CH)])
        s_norms = sems(nc, ctx, pre, "xn", "xn2")
        s_stats = sems(nc, ctx, pre, "stats1", "stats2")
        block = ctx.enter_context(nc.Block())
        n_st = 1

        @block.sync
        def _(sp):
            if L == 0:
                for c in range(CH):
                    sp.dma_start(x_sb[:, 8 * c:8 * c + 8, :], x_view[:, 8 * c:8 * c + 8, :]).then_inc(s_x[c], 16)
                sp.wait_ge(s_norms[0], NT)
                sp.dma_start(io["xn_store"], x_sb).then_inc(s_st, 16)
                sp.wait_ge(s_fr, NT + 2)
                sp.dma_start(io["xT_store"], xTf).then_inc(s_st, 16)
                sp.wait_ge(s_st, 32)
            else:
                sp.wait_ge(s_fr2, NT + 2)
                sp.wait_ge(s_fr, NT + 2)
                sp.dma_start(io["xT_store"], xTa).then_inc(s_st, 16)
                sp.wait_ge(s_st, 16)

        @block.vector
        def _(dve):
            link = Chain(dve, s_dve)
            dve.sem_inc(s_fr2, 2)
            for r in range(norms):
                src, dst = (x_sb, x_sb) if r == 0 else (x_sb, x2_sb)
                for c in range(CH):
                    if L == 0 and r == 0:
                        dve.wait_ge(s_x[c], 16)
                    with dve.Fori(0, 8) as t:
                        nc.vector.bn_stats(stats[:, 8 * c + t, :], src[:, 8 * c + t, :]).then_inc(s_stats[r], 1)
                dve.wait_ge(s_stats[r], NT)
                st, sm = stats, m.small
                link(nc.vector.tensor_tensor(sm[:, MEAN, :], st[:, :, 1], st[:, :, 4], ALU.add))
                link(nc.vector.tensor_scalar(sm[:, MEAN, :], sm[:, MEAN, :], 0.5, None, ALU.mult))
                link(nc.vector.tensor_tensor(sm[:, T0, :], st[:, :, 1], st[:, :, 4], ALU.subtract))
                link(nc.vector.scalar_tensor_tensor(sm[:, T0, :], sm[:, T0, :], 0.25, sm[:, T0, :],
                                                    ALU.mult, ALU.mult))
                link(nc.vector.tensor_tensor(sm[:, T1, :], st[:, :, 2], st[:, :, 5], ALU.add))
                link(nc.vector.scalar_tensor_tensor(sm[:, VAR, :], sm[:, T1, :], 1.0 / D, sm[:, T0, :],
                                                    ALU.mult, ALU.add))
                nc.vector.tensor_scalar(sm[:, VAR, :], sm[:, VAR, :], LN_EPS, None, ALU.add).then_inc(s_var, 1)
                dve.wait_ge(s_std, r + 1)
                link(nc.vector.reciprocal(sm[:, RSTD, :], sm[:, T1, :]))
                with dve.Fori(0, NT) as t:
                    nc.vector.tensor_scalar(dst[:, t, :], src[:, t, :], sm[:, MEAN, bass.ds(t, 1)],
                                            sm[:, RSTD, bass.ds(t, 1)], ALU.subtract, ALU.mult).then_inc(s_norms[r], 1)
                if r == 0 and norms == 2:
                    dve.wait_ge(s_norms[0], NT)
            with dve.Fori(0, NT // 2) as i:
                for par in range(2):
                    t = 2 * i + par
                    dve.wait_ge(s_tr, t + 1)
                    ps = m.psS[par]
                    if L == 0:
                        nc.vector.tensor_copy(xTa[:, :, bass.ds(t * P, P)],
                                              ps[:, 512:768].rearrange("p (k t) -> p k t", k=KD)).then_inc(s_fr2, 1)
                    else:
                        nc.vector.tensor_copy(xTa[:, 0, bass.ds(t * P, P)], ps[:, 0:P]).then_inc(s_fr2, 1)

        @block.scalar
        def _(act):
            act.sem_inc(s_fr, 2)
            for r in range(norms):
                act.wait_ge(s_var, r + 1)
                nc.scalar.activation(m.small[:, T1, :], m.small[:, VAR, :], ACT.Sqrt).then_inc(s_std, 1)
            with act.Fori(0, NT // 2) as i:
                for par in range(2):
                    t = 2 * i + par
                    act.wait_ge(s_tr, t + 1)
                    ps = m.psS[par]
                    if L == 0:
                        nc.scalar.activation(xTf[:, :, bass.ds(t * P, P)],
                                             ps[:, 0:256].rearrange("p (k t) -> p k t", k=KD), ACT.Copy)\
                            .then_inc(s_fr, 1)
                    else:
                        nc.scalar.activation(xTa[:, 1, bass.ds(t * P, P)], ps[:, 512:512 + P], ACT.Copy)\
                            .then_inc(s_fr, 1)

        @block.tensor
        def _(pe):
            for i in range(NT // 2):
                for par in range(2):
                    t = 2 * i + par
                    ps = m.psS[par]
                    pe.wait_ge(s_norms[norms - 1], t + 1)
                    pe.wait_ge(s_fr, t + 1)
                    pe.wait_ge(s_fr2, t + 1)
                    if L == 0:
                        for k in range(KD):
                            nc.tensor.transpose(ps[:, k * P:(k + 1) * P], x_sb[:, t, k * P:(k + 1) * P], m.ident[:, :])
                        for k in range(KD):
                            last = nc.tensor.transpose(ps[:, 512 + k * P:512 + (k + 1) * P],
                                                       x2_sb[:, t, k * P:(k + 1) * P], m.ident[:, :])
                    else:
                        for k in range(KD):
                            last = nc.tensor.transpose(ps[:, 512 * k:512 * k + P], x_sb[:, t, k * P:(k + 1) * P],
                                                       m.ident[:, :])
                    last.then_inc(s_tr, 1)


def split_parts(nc, link, src, parts, rest, before_last):
    link(nc.vector.tensor_copy(parts[:, 0, :], src))
    link(nc.vector.tensor_tensor(rest, src, parts[:, 0, :], ALU.subtract))
    link(nc.vector.tensor_copy(parts[:, 1, :], rest))
    return nc.vector.tensor_tensor(parts[:, 2, :], rest, parts[:, 1, :], ALU.subtract)


def projection_phase(nc, m, io, L):
    pre = f"p{L}"
    xTa = m.area(2 * NT * D, KD, B * T)
    vg_w = 2 * D if L == 0 else D
    wqk = m.area(0, KD, 2 * D)
    wvg = m.area(1024, KD, vg_w)
    bqk = m.area(2048, NQK)
    bvg = m.area(2052, 2 * D)
    bvg_all = m.area(2600, 2 * D)
    sel = m.area(3200, NQK, 2 * HEADS)
    selT = m.area(3400, NQK, P)
    proj = m.area(4096, NQK, 512)
    sq = m.area(6144, 2, 512)
    rest = m.area(7168, 512)
    parts = [m.work[:, 8192 + 768 * i:8192 + 768 * (i + 1)].bitcast(BF16).rearrange("p (a t) -> p a t", a=3)
             for i in range(2)]
    n_sb = m.area(9728, 512)
    n_rest = m.area(10240, 512)
    n_parts = m.work[:, 10752:11520].bitcast(BF16).rearrange("p (a t) -> p a t", a=3)
    r_norm = m.area(11520, 512)
    NR = 2 * HEADS
    n_loads = 6 if L == 0 else 4
    with ExitStack() as ctx:
        (s_load, s_dve, s_bias, s_bias_row, s_proj, s_P, s_sq, s_nm, s_nsb, s_nparts, s_nst, s_vps, s_vfree, s_rn,
         s_e, s_efree, s_parts, s_v) = sems(
            nc, ctx, pre, "load", "dve", "bias", "bias_rows", "proj", "projected", "squared", "norm_mm", "norm_copied",
            "norm_parts", "norm_stored", "v_ready", "v_free", "rnorm", "expanded", "expand_free", "parts",
            "values")
        s_st = sems(nc, ctx, pre, "stored0", "stored1")
        block = ctx.enter_context(nc.Block())

        @block.sync
        def _(sp):
            sp.dma_start(wqk, io["wqk"].rearrange("(k p) n -> p k n", p=P)).then_inc(s_load, 16)
            sp.dma_start(wvg, io["wvg"].rearrange("(k p) n -> p k n", p=P)).then_inc(s_load, 16)
            sp.dma_start(sel, io["sel"].rearrange("p (f r) -> p f r", f=NQK)).then_inc(s_load, 16)
            sp.dma_start(selT[0:NR], io["selT"].rearrange("p (f r) -> p f r", f=NQK)).then_inc(s_load, 16)
            if L == 0:
                sp.dma_start(bqk, io["bqk"]).then_inc(s_load, 16)
                sp.dma_start(bvg[0:1, :], io["bvg"]).then_inc(s_load, 16)
            with sp.Fori(0, TB) as i:
                for ft in range(NQK):
                    sp.wait_ge(s_parts, 4 * i + ft + 5)
                    sp.dma_start(io["qk_parts"][:, ft * P:(ft + 1) * P, bass.ds(i * 512, 512)]
                                 .rearrange("a p t -> p a t"), parts[ft % 2]).then_inc(s_st[ft % 2], 16)
                if L == 0:
                    sp.wait_ge(s_nparts, i + 2)
                    sp.dma_start(io["norm_parts"][:, :, bass.ds(i * 512, 512)].rearrange("a p t -> p a t"),
                                 n_parts[0:NR]).then_inc(s_nst, 16)
            for x in s_st:
                sp.wait_ge(x, 16 * (2 * TB + 1))
            if L == 0:
                sp.wait_ge(s_nst, 16 * (TB + 1))

        @block.tensor
        def _(pe):
            pe.sem_inc(s_nm, 2)
            pe.wait_ge(s_load, 16 * n_loads)
            if L == 0:
                nc.tensor.matmul(m.psM[0][:, :], m.ones_row[0:1, :], bvg[0:1, :], start=True, stop=True)\
                    .then_inc(s_bias_row, 1)
                pe.wait_ge(s_bias, 2)

            def norm(i, ft):
                pe.wait_ge(s_sq, 4 * i + ft + 1)
                if ft == 0:
                    pe.wait_ge(s_nsb, i + 1)
                nc.tensor.matmul(m.psO[0][0:NR, :], sel[:, ft, :], sq[:, ft % 2, :], start=ft == 0,
                                 stop=ft == NQK - 1).then_inc(s_nm, 1)

            for i in range(TB):
                for ft in range(NQK):
                    pe.wait_ge(s_P, 4 * i + ft + 1)
                    for k in range(KD):
                        last = nc.tensor.matmul(m.psS[ft % 2][:, 0:512], wqk[:, k, ft * P:(ft + 1) * P],
                                                xTa[:, k, bass.ds(i * 512, 512)], start=k == 0, stop=k == KD - 1)
                    last.then_inc(s_proj, 1)
                    if ft > 0:
                        norm(i, ft - 1)
                for tt in range(4):
                    pe.wait_ge(s_vfree, 4 * i + tt + 1)
                    for k in range(KD):
                        last = nc.tensor.matmul(m.psM[tt % 2][:, 0:vg_w], xTa[:, k, bass.ds(i * 512 + tt * P, P)],
                                                wvg[:, k, :], start=k == 0, stop=k == KD - 1)
                    last.then_inc(s_vps, 1)
                    if tt == 0:
                        norm(i, NQK - 1)
                if L == 1:
                    pe.wait_ge(s_rn, i + 2)
                    for ft in range(NQK):
                        pe.wait_ge(s_efree, 4 * i + ft + 1)
                        nc.tensor.matmul(m.psO[1][:, :], selT[0:NR, ft, :], r_norm[0:NR, :], start=True, stop=True)\
                            .then_inc(s_e, 1)

        @block.scalar
        def _(act):
            act.sem_inc(s_P, 2)
            act.sem_inc(s_nsb, 1)
            if L == 0:
                act.wait_ge(s_bias, 2)
            with act.Fori(0, TB) as i:
                for ft in range(NQK):
                    act.wait_ge(s_proj, 4 * i + ft + 1)
                    act.wait_ge(s_parts, 4 * i + ft + 1)
                    if L == 0:
                        nc.scalar.activation(proj[:, ft, :], m.psS[ft % 2][:, 0:512], ACT.Identity,
                                             bias=bqk[:, ft:ft + 1], scale=-2.0 if ft < 2 else 1.0).then_inc(s_P, 1)
                    else:
                        nc.scalar.activation(proj[:, ft, :], m.psS[ft % 2][:, 0:512], ACT.Copy).then_inc(s_P, 1)
                    act.wait_ge(s_P, 4 * i + ft + 3)
                    act.wait_ge(s_nm, 4 * i + ft + 1)
                    nc.scalar.activation(sq[:, ft % 2, :], proj[:, ft, :], ACT.Square,
                                         scale=0.5 if L == 0 and ft < 2 else 1.0).then_inc(s_sq, 1)
                act.wait_ge(s_nm, 4 * i + 6)
                if L == 0:
                    act.wait_ge(s_nparts, i + 1)
                else:
                    act.wait_ge(s_rn, i + 1)
                nc.scalar.activation(n_sb[0:NR, :], m.psO[0][0:NR, :], ACT.Copy if L == 0 else ACT.Sqrt)\
                    .then_inc(s_nsb, 1)

        @block.vector
        def _(dve):
            dve.sem_inc(s_parts, 4)
            dve.sem_inc(s_vfree, 2)
            dve.sem_inc(s_efree, 1)
            dve.sem_inc(s_nparts, 1)
            dve.sem_inc(s_rn, 1)
            for x in s_st + [s_nst]:
                dve.sem_inc(x, 16)
            per_block = NQK * (3 if L == 0 else 3) + (3 if L == 0 else 1)
            chain_n = [0]
            dve.wait_ge(s_load, 16 * n_loads)
            if L == 0:
                nc.vector.tensor_scalar(bqk[:, 0:2], bqk[:, 0:2], -2.0, None, ALU.mult).then_inc(s_bias, 1)
                dve.wait_ge(s_bias_row, 1)
                nc.vector.tensor_copy(bvg_all, m.psM[0][:, :]).then_inc(s_bias, 1)
                dve.wait_ge(s_bias, 2)
            with dve.Fori(0, TB) as i:
                chain_n[0] = 0

                def link(ins):
                    chain_n[0] += 1
                    ins.then_inc(s_dve, 1)
                    dve.wait_ge(s_dve, per_block * i + chain_n[0])

                def split(ft):
                    dve.wait_ge(s_st[ft % 2], 32 * i + 16 * (ft // 2) + 16)
                    split_parts(nc, link, proj[:, ft, :], parts[ft % 2], rest, None).then_inc(s_parts, 1)
                    dve.wait_ge(s_parts, 4 * i + ft + 5)

                def value_tile(tt):
                    dve.wait_ge(s_vps, 4 * i + tt + 1)
                    t = 4 * i + tt
                    ps = m.psM[tt % 2]
                    if L == 0:
                        nc.vector.tensor_tensor(m.values[:, t, :], ps[:, 0:D], bvg_all[:, 0:D], ALU.add)\
                            .then_inc(s_v, 1)
                        nc.vector.tensor_tensor(m.gated[:, t, :], ps[:, D:2 * D], bvg_all[:, D:2 * D], ALU.add)\
                            .then_inc(s_vfree, 1)
                    else:
                        nc.vector.tensor_copy(m.values[:, t, :], ps[:, 0:D]).then_inc(s_vfree, 1)

                if L == 0:
                    for ft in range(NQK):
                        dve.wait_ge(s_P, 4 * i + ft + 3)
                        split(ft)
                        value_tile(ft)
                    dve.wait_ge(s_nsb, i + 2)
                    dve.wait_ge(s_nst, 16 * i + 16)
                    split_parts(nc, link, n_sb[0:NR, :], n_parts[0:NR], n_rest[0:NR, :], None).then_inc(s_nparts, 1)
                else:
                    for tt in range(4):
                        value_tile(tt)
                    dve.wait_ge(s_nsb, i + 2)
                    link(nc.vector.tensor_scalar(n_rest[0:NR, :], n_sb[0:NR, :], NORM_EPS, None, ALU.max))
                    nc.vector.reciprocal(r_norm[0:NR, :], n_rest[0:NR, :]).then_inc(s_rn, 1)
                    for ft in range(NQK):
                        dve.wait_ge(s_e, 4 * i + ft + 1)
                        nc.vector.tensor_tensor(proj[:, ft, :], m.psO[1][:, :], proj[:, ft, :], ALU.mult)\
                            .then_inc(s_efree, 1)
                        dve.wait_ge(s_efree, 4 * i + ft + 2)
                        split(ft)


def attention_phase(nc, m, io, L):
    pre = f"a{L}"
    UNITS = KT * B
    RING = 8
    ring = m.area(0, RING, T)
    q_ring = m.area(RING * T, 4, T)
    LAG_PV = 5
    LAG_INV, LAG_SQ = 2, 3
    ACT_POW = 1664
    POW_STEPS = 5
    BATCH = 4
    ACT_SQ = 1024
    rows = ROWS + NORM_ROWS if L == 0 else ROWS
    loads = 2 * len(PRODUCTS) + (2 if L == 0 else 0)
    values = m.values[:, :, :].rearrange("p (b k) (h d) -> p b k h d", b=B, h=HEADS)
    gated = m.gated[:, :, :].rearrange("p (b q a) (h d) -> p b q a h d", b=B, q=QB, h=HEADS)
    EPS_SUM = SHEP_EPS if L == 0 else SUM_EPS1
    with ExitStack() as ctx:
        (s_qk, s_pv, s_fin, s_h, s_r, s_yps, s_yo, s_yst, s_o, s_ot, s_den, s_rec, s_g, s_vt) = sems(
            nc, ctx, pre, "scores", "pv", "ffn_loaded", "ffn_hidden", "ffn_relu", "ffn_sum", "ffn_copied",
            "ffn_stored", "out_copied", "out_transposed", "den", "rec", "gated", "v_tile")
        if L == 0:
            s_a, s_y, s_m, s_v, s_wa, s_wd, s_r2, s_g0 = sems(
                nc, ctx, pre, "inv_dist", "quot", "guarded", "inv_shifted", "w_act", "w_dve", "ffn_squared", "gated0")
        else:
            s_cl, s_q, s_rs, s_ls, s_z, s_at, s_ln, s_w, s_pw = sems(
                nc, ctx, pre, "clipped", "cos2", "rsin", "log_sin", "tan_half", "angle", "log", "w_act", "w_dve")
        s_stk = sems(nc, ctx, pre, "stack0", "stack1")
        block = ctx.enter_context(nc.Block())

        def pairs(eng, body):
            body(0, True, False)
            with eng.Fori(1, HEADS - 1) as h:
                body(h, False, False)
            body(HEADS - 1, False, True)

        @block.sync
        def _(sp):
            def head(h, first, last):
                for b in range(B):
                    if not first:
                        sp.wait_ge(s_qk, 2 * (UNITS * h + KT * b + KT - UNITS))
                    tok = slice(b * T, (b + 1) * T)
                    for side, stack in ((0, m.q_stack[b]), (1, m.k_stack[b])):
                        for g, pr in enumerate(PRODUCTS):
                            sp.dma_start(stack[g * DH:(g + 1) * DH, :],
                                         io["qk_parts"][pr[side], bass.ds(h * DH + side * D, DH), tok])\
                                .then_inc(s_stk[b], 16)
                        if L == 0:
                            at = ROWS + 3 * side
                            sp.dma_start(stack[at:at + 3, :],
                                         io["norm_parts"][:, bass.ds(h + HEADS * side, 1), tok]
                                         .rearrange("a o t -> (a o) t")).then_inc(s_stk[b], 16)
                    if not (first and b == 0):
                        sp.wait_ge(s_h, 2 * (2 * h + b))
                    sp.dma_start(m.ffn_in[:, :, :], io["xT_store"][:, :, bass.ds((2 * h + b) * P, P)])\
                        .then_inc(s_fin, 16)
            pairs(sp, head)

        @block.gpsimd
        def _(pool):
            def head(h, first, last):
                for b in range(B):
                    if not first:
                        pool.wait_ge(s_pv, UNITS * h + KT * b + KT - UNITS)
                    nc.gpsimd.tensor_copy(m.v_tile[b][:, :, 0:DH], values[:, b, :, h, :]).then_inc(s_vt, 1)
            pairs(pool, head)

        def pe_scores(pe, h, u, first, halves=(0, 1)):
            b, kt = u // KT, u % KT
            if kt == 0 and halves[0] == 0:
                pe.wait_ge(s_stk[b], 16 * loads * (h + 1))
            for half in halves:
                if not (first and u == 0):
                    pe.wait_ge(s_y if L == 0 else s_cl, 2 * (UNITS * h + u) + half - 1)
                for q in range(2):
                    c = (2 * half + q) * 512
                    last = nc.tensor.matmul(m.psS[half][:, q * 512:(q + 1) * 512],
                                            m.k_stack[b][0:rows, kt * P:(kt + 1) * P],
                                            m.q_stack[b][0:rows, c:c + 512], start=True, stop=True)
                last.then_inc(s_qk, 1)

        def pe_values(pe, h, u, first, blocks=range(QB)):
            n = UNITS * h + u
            b, kt = (u % UNITS) // KT, u % KT
            if blocks[0] == 0:
                if kt == 0:
                    pe.wait_ge(s_vt, 2 * h + (u // KT) + 1)
                    if not (first and 0 <= u < UNITS):
                        pe.wait_ge(s_o, 2 * h + (u // KT) - 1)
                if L == 0:
                    pe.wait_ge(s_wa, n + 1)
                    pe.wait_ge(s_wd, n + 1)
                else:
                    pe.wait_ge(s_w, n + 1)
                    pe.wait_ge(s_pw, POW_STEPS * (UNITS // BATCH * h + u // BATCH + 1))
            for q in blocks:
                last = nc.tensor.matmul(m.psO[b][VW * q:VW * (q + 1), :], m.v_tile[b][:, kt, :],
                                        ring[:, u % RING, q * 512:(q + 1) * 512], start=kt == 0, stop=kt == KT - 1)
            if blocks[-1] == QB - 1:
                last.then_inc(s_pv, 1)

        def pe_out(pe, n):
            pe.wait_ge(s_o, n + 1)
            for a in range(4):
                last = nc.tensor.transpose(m.psM[1][:, a * P:(a + 1) * P], m.head_outT[:, a * P:(a + 1) * P],
                                           m.ident[:, :])
            last.then_inc(s_ot, 1)

        def pe_hidden(pe, n, very_first, quarters=range(4)):
            for quarter in quarters:
                if quarter == 0:
                    pe.wait_ge(s_fin, 16 * (n + 1))
                    if not very_first:
                        pe.wait_ge(s_yo, n)
                if quarter == 2 and not very_first:
                    pe.wait_ge(s_g, n)
                g = quarter // 2
                for f in range(2 * (quarter % 2), 2 * (quarter % 2) + 2):
                    for k in range(KD):
                        c = (4 * g + f) * P
                        last = nc.tensor.matmul(m.psM[g][:, f * P:(f + 1) * P], m.w1T[:, k, c:c + P],
                                                m.ffn_in[:, k, :], start=k == 0 and (L == 0 or f == 0),
                                                stop=L == 0 and k == KD - 1)
                if quarter % 2 == 0:
                    continue
                if L == 1:
                    last = nc.tensor.matmul(m.psM[g][:, :], m.b1_tiles[:, :],
                                            m.ident[0:FT, 4 * g:4 * g + 4].unsqueeze(2).broadcast_to([FT, 4, P]),
                                            start=False, stop=True)
                last.then_inc(s_h, 1)

        def pe_ffn_sum(pe, n, fs=range(FT)):
            if fs[0] == 0:
                pe.wait_ge(s_r if L == 1 else s_r2, 2 * (n + 1) if L == 1 else n + 1)
            for f in fs:
                last = nc.tensor.matmul(m.psM[0][:, 0:D], m.hidden[:, f, :], m.w2T[:, f, :], start=f == 0,
                                        stop=L == 0 and f == FT - 1)
            if L == 1:
                last = nc.tensor.matmul(m.psM[0][:, 0:D], m.ones_row[0:1, :], m.b2_row[0:1, :], start=False, stop=True)
            if fs[-1] == FT - 1:
                last.then_inc(s_yps, 1)

        def act_out(act, n, b):
            act.wait_ge(s_pv, KT * (n + 1))
            act.wait_ge(s_ot, n)
            nc.scalar.activation(m.head_outT[:, :], m.psO[b][:, :], ACT.Copy).then_inc(s_o, 1)

        def act_relu(act, n, groups=range(2)):
            act.wait_ge(s_yps, n)
            for g in groups:
                act.wait_ge(s_h, 2 * n + g + 1)
                nc.scalar.activation(m.hidden[:, 4 * g:4 * g + 4, :], m.psM[g][:, :].rearrange("p (f t) -> p f t", f=4),
                                     ACT.Relu).then_inc(s_r, 1)

        def act_ffn_out(act, n):
            act.wait_ge(s_yps, n + 1)
            act.wait_ge(s_yst, 16 * n)
            nc.scalar.activation(m.ffn_out[:, :], m.psM[0][:, 0:D], ACT.Copy).then_inc(s_yo, 1)
            act.wait_ge(s_yo, n + 1)
            act.dma_start(io["y_store"][bass.ds(n, 1), :, :].rearrange("o p d -> (o p) d"), m.ffn_out[:, :])\
                .then_inc(s_yst, 16)

        def dve_out(dve, h, b, n):
            dve.wait_ge(s_ot, n + 1)
            ps = m.psM[1][:, :].rearrange("p (a q c) -> p q a c", a=4, q=QB)
            den = m.den[:, 0, :].rearrange("p (q a) -> p q a", q=QB)
            rec = m.den[:, 1, :].rearrange("p (q a) -> p q a", q=QB)
            nc.vector.tensor_scalar(den, ps[:, :, :, DH], EPS_SUM, None, ALU.add).then_inc(s_den, 1)
            dve.wait_ge(s_den, n + 1)
            nc.vector.reciprocal(m.den[:, 1, :], m.den[:, 0, :]).then_inc(s_rec, 1)
            dve.wait_ge(s_rec, n + 1)
            out = gated[:, b, :, :, h, :]
            rec16 = rec.unsqueeze(3).broadcast_to([P, QB, 4, DH])
            if L == 0:
                nc.vector.tensor_tensor(out, ps[:, :, :, 0:DH], out, ALU.mult).then_inc(s_g0, 1)
                dve.wait_ge(s_g0, n + 1)
                nc.vector.tensor_tensor(out, out, rec16, ALU.mult).then_inc(s_g, 1)
            else:
                nc.vector.tensor_tensor(out, ps[:, :, :, 0:DH], rec16, ALU.mult).then_inc(s_g, 1)

        if L == 0:
            OUT_COPY, OUT_T, OUT_DIV = 5, 6, 7
            HID = (2, 3, 8, 9)
            RELU = (6, 10)
            SQ, COPY = 11, 15
            SUM = {12: (0, 1, 2), 13: (3, 4, 5), 14: (6, 7)}

            @block.tensor
            def _(pe):
                def head(h, first, last):
                    for u in range(UNITS + (LAG_PV if last else 0)):
                        b, kt = u // KT, u % KT
                        n = 2 * h + b
                        if u < UNITS:
                            pe_scores(pe, h, u, first, (0,))
                        if not (first and u < LAG_PV):
                            pe_values(pe, h, u - LAG_PV, first)
                        if u < UNITS:
                            pe_scores(pe, h, u, first, (1,))
                        if kt == OUT_T and not (first and b == 0):
                            pe_out(pe, n - 1)
                        if kt in HID and u < UNITS:
                            pe_hidden(pe, n, first and b == 0, (HID.index(kt),))
                        if kt in SUM:
                            pe_ffn_sum(pe, n, SUM[kt])
                    if last:
                        pe_out(pe, 2 * HEADS - 1)
                pairs(pe, head)

            @block.scalar
            def _(act):
                def head(h, first, last):
                    def inverse_distance(u, half):
                        c = UNITS * h + u
                        if half == 0 and not (first and u < RING):
                            act.wait_ge(s_pv, c - RING + 1)
                        act.wait_ge(s_qk, 2 * c + half + 1)
                        nc.scalar.activation(ring[:, u % RING, half * 1024:(half + 1) * 1024],
                                             m.psS[half][:, :], ACT.Abs_reciprocal_sqrt).then_inc(s_a, 1)

                    for u in range(UNITS + (LAG_SQ if last else 0)):
                        b, kt = u // KT, u % KT
                        n = 2 * h + b
                        c = UNITS * h + u
                        if u < UNITS:
                            inverse_distance(u, 0)
                        if u < UNITS + LAG_INV and not (first and u < LAG_INV):
                            act.wait_ge(s_m, c - LAG_INV + 1)
                            slot = ring[:, (u - LAG_INV) % RING, :]
                            nc.scalar.activation(slot, slot, ACT.Abs_reciprocal_sqrt, bias=SHEP_EPS * SHEP_EPS,
                                                 scale=2 * SHEP_EPS).then_inc(s_v, 1)
                        if u < UNITS:
                            inverse_distance(u, 1)
                        if not (first and u < LAG_SQ):
                            act.wait_ge(s_v, c - LAG_SQ + 1)
                            slot = ring[:, (u - LAG_SQ) % RING, 0:ACT_SQ]
                            nc.scalar.activation(slot, slot, ACT.Square).then_inc(s_wa, 1)
                        if kt == OUT_COPY and not (first and b == 0) and u < UNITS:
                            act_out(act, n - 1, (b + 1) % 2)
                        if kt in RELU:
                            act_relu(act, n, (RELU.index(kt),))
                        if kt == COPY:
                            act_ffn_out(act, n)
                    if last:
                        act_out(act, 2 * HEADS - 1, 1)
                        act.wait_ge(s_yst, 16 * 2 * HEADS)
                pairs(act, head)

            @block.vector
            def _(dve):
                def head(h, first, last):
                    def quotient(u, half):
                        c = UNITS * h + u
                        dve.wait_ge(s_a, 2 * c + half + 1)
                        part = ring[:, u % RING, half * 1024:(half + 1) * 1024]
                        nc.vector.scalar_tensor_tensor(part, part, 0.5 / SHEP_EPS, m.psS[half][:, :],
                                                       ALU.add, ALU.mult).then_inc(s_y, 1)

                    for u in range(UNITS + (LAG_SQ if last else 0)):
                        b, kt = u // KT, u % KT
                        n = 2 * h + b
                        c = UNITS * h + u
                        if u < UNITS:
                            quotient(u, 0)
                        if u <= UNITS and not (first and u < 1):
                            dve.wait_ge(s_y, 2 * c)
                            slot = ring[:, (u - 1) % RING, :]
                            nc.vector.tensor_scalar(slot, slot, 0.0, None, ALU.max).then_inc(s_m, 1)
                        if u < UNITS:
                            quotient(u, 1)
                        if not (first and u < LAG_SQ):
                            dve.wait_ge(s_v, c - LAG_SQ + 1)
                            part = ring[:, (u - LAG_SQ) % RING, ACT_SQ:T]
                            nc.vector.tensor_tensor(part, part, part, ALU.mult).then_inc(s_wd, 1)
                        if kt == OUT_DIV and not (first and b == 0) and u < UNITS:
                            dve_out(dve, h if b else h - 1, 1 - b, n - 1)
                        if kt == SQ:
                            dve.wait_ge(s_r, 2 * n + 2)
                            nc.vector.tensor_tensor(m.hidden[:, :, :], m.hidden[:, :, :], m.hidden[:, :, :],
                                                    ALU.mult).then_inc(s_r2, 1)
                    if last:
                        dve_out(dve, HEADS - 1, 1, 2 * HEADS - 1)
                pairs(dve, head)
        else:
            NB = UNITS // BATCH

            @block.tensor
            def _(pe):
                def head(h, first, last):
                    for j in range(NB + (1 if last else 0)):
                        n = 2 * h + j // 4
                        if first and j == 0:
                            pe_scores(pe, h, 0, True)
                        for u in range(BATCH * j + 1, min(BATCH * (j + 1) + 1, UNITS)):
                            pe_scores(pe, h, u, first)
                        if j == NB - 1 and not last:
                            pe_scores(pe, h + 1, 0, False)
                        if not (first and j == 0):
                            for u in range(BATCH * (j - 1), BATCH * j):
                                pe_values(pe, h, u, first)
                        if j % 4 == 1 and not (first and j < 4):
                            pe_out(pe, n - 1)
                        if j % 4 == 2:
                            pe_hidden(pe, n, first and j < 4)
                        if j % 4 == 3:
                            pe_ffn_sum(pe, n)
                    if last:
                        pe_out(pe, 2 * HEADS - 1)
                pairs(pe, head)

            @block.scalar
            def _(act):
                def head(h, first, last):
                    for j in range(NB):
                        n = 2 * h + j // 4
                        twos = [(BATCH * j + 2 * i, BATCH * j + 2 * i + 1) for i in range(BATCH // 2)]
                        if j == 0:
                            nc.scalar.preload_act_table_set("natural_log_exp_and_others")
                        for u, v in twos:
                            act.wait_ge(s_q, UNITS * h + v + 1)
                            pair = q_ring[:, u % BATCH:u % BATCH + 2, :]
                            nc.scalar.activation(pair, pair, ACT.Ln, bias=1.0, scale=-1.0).then_inc(s_ls, 1)
                        for u in range(BATCH * j, BATCH * (j + 1)):
                            act.wait_ge(s_ls, UNITS // 2 * h + u // 2 + 1)
                            slot = q_ring[:, u % BATCH, :]
                            nc.scalar.activation(slot, slot, ACT.Sigmoid, scale=-0.5).then_inc(s_rs, 1)
                        for u, v in twos:
                            act.wait_ge(s_z, UNITS * h + v + 1)
                            pair = ring[:, u % RING:u % RING + 2, :]
                            nc.scalar.activation(pair, pair, ACT.Arctan).then_inc(s_at, 1)
                        nc.scalar.preload_act_table_set("natural_log_exp_and_others")
                        for u, v in twos:
                            act.wait_ge(s_at, UNITS // 2 * h + u // 2 + 1)
                            pair = ring[:, u % RING:u % RING + 2, 0:ACT_POW]
                            nc.scalar.activation(pair, pair, ACT.Ln, bias=0.5, scale=2.0 / PI)\
                                .then_inc(s_ln, 1)
                        for u, v in twos:
                            act.wait_ge(s_ln, UNITS // 2 * h + u // 2 + 1)
                            pair = ring[:, u % RING:u % RING + 2, 0:ACT_POW]
                            nc.scalar.activation(pair, pair, ACT.Exp, scale=16.0).then_inc(s_w, 2)
                        if j % 4 == 0 and not (first and j == 0):
                            act_out(act, n - 1, (j // 4 + 1) % 2)
                        if j % 4 == 2:
                            act_relu(act, n)
                        if j % 4 == 3:
                            act_ffn_out(act, n)
                    if last:
                        act_out(act, 2 * HEADS - 1, 1)
                        act.wait_ge(s_yst, 16 * 2 * HEADS)
                pairs(act, head)

            @block.vector
            def _(dve):
                def head(h, first, last):
                    def cosines(u):
                        c = UNITS * h + u
                        if not (first and u < RING):
                            dve.wait_ge(s_pv, c - RING + 1)
                        for half in range(2):
                            dve.wait_ge(s_qk, 2 * c + half + 1)
                            nc.vector.tensor_scalar(ring[:, u % RING, half * 1024:(half + 1) * 1024],
                                                    m.psS[half][:, :], COS_MAX, -COS_MAX, ALU.min, ALU.max)\
                                .then_inc(s_cl, 1)

                    def square_cosines(u):
                        c = UNITS * h + u
                        dve.wait_ge(s_cl, 2 * c + 2)
                        nc.vector.tensor_tensor(q_ring[:, u % BATCH, :], ring[:, u % RING, :], ring[:, u % RING, :],
                                                ALU.mult).then_inc(s_q, 1)

                    def powers(j):
                        dve.wait_ge(s_at, UNITS // 2 * h + 2 * j + 2)
                        first_slot = (BATCH * j) % RING
                        part = ring[:, first_slot:first_slot + BATCH, ACT_POW:T]
                        done = POW_STEPS * (NB * h + j)
                        nc.vector.tensor_scalar(part, part, 2.0 / PI, 0.5, ALU.mult, ALU.add).then_inc(s_pw, 1)
                        for i in range(1, POW_STEPS):
                            dve.wait_ge(s_pw, done + i)
                            nc.vector.tensor_tensor(part, part, part, ALU.mult).then_inc(s_pw, 1)

                    for j in range(NB + (1 if last else 0)):
                        n = 2 * h + j // 4
                        us = range(BATCH * j, BATCH * (j + 1))
                        if j < NB:
                            cosines(us[0])
                            cosines(us[1])
                            square_cosines(us[0])
                            square_cosines(us[1])
                            cosines(us[2])
                            cosines(us[3])
                            square_cosines(us[2])
                            square_cosines(us[3])
                        if not (first and j == 0):
                            powers(j - 1)
                        if j < NB:
                            for u in us:
                                dve.wait_ge(s_rs, UNITS * h + u + 1)
                                slot = ring[:, u % RING, :]
                                nc.vector.tensor_tensor(slot, slot, q_ring[:, u % BATCH, :], ALU.mult).then_inc(s_z, 1)
                            dve.wait_ge(s_z, UNITS * h + BATCH * (j + 1))
                        if j < NB and j % 4 == 1 and not (first and j < 4):
                            dve_out(dve, h if j >= 4 else h - 1, (j // 4 + 1) % 2, n - 1)
                    if last:
                        dve_out(dve, HEADS - 1, 1, 2 * HEADS - 1)
                pairs(dve, head)


def output_phase(nc, m, io, L):
    pre = f"o{L}"
    x_sb = m.area(0, NT, D)
    xn_sb = m.area(NT * D, NT, D)
    g_sb = m.area(2 * NT * D, NT, D)
    woT = m.hidden[:, 0:4, :].rearrange("p (k a) b -> p k (a b)", k=KD)
    bo = m.ffn_out[0:1, :]
    oT = [m.w1T[:, i, 0:D].rearrange("p (k t) -> p k t", k=KD) for i in range(2)]
    tmp = [m.w2T[:, i, :] for i in range(2)]
    CH = 4
    with ExitStack() as ctx:
        s_load, s_y, s_silu, s_tr, s_oT, s_mm, s_free, s_s, s_sg, s_x, s_st = sems(
            nc, ctx, pre, "load", "y", "silu", "transposed", "copied", "product", "free", "s", "sg", "x", "stored")
        block = ctx.enter_context(nc.Block())
        n_loads = 4 if L == 0 else 3
        x_view = (io["x"] if L == 0 else io["x1_store"]).rearrange("(t p) d -> p t d", p=P)
        out_view = (io["x1_store"] if L == 0 else io["out"]).rearrange("(t p) d -> p t d", p=P)

        @block.sync
        def _(sp):
            sp.dma_start(g_sb, io["y_store"].rearrange("t p d -> p t d")).then_inc(s_y, 16)
            sp.dma_start(woT, io["woT"].rearrange("(k p) n -> p k n", p=P)).then_inc(s_load, 16)
            sp.dma_start(bo, io["bo"]).then_inc(s_load, 16)
            sp.dma_start(x_sb, x_view).then_inc(s_load, 16)
            if L == 0:
                sp.dma_start(xn_sb, io["xn_store"]).then_inc(s_load, 16)
            for c in range(CH):
                sp.wait_ge(s_x, 8 * (c + 1) + 1)
                sp.dma_start(out_view[:, 8 * c:8 * c + 8, :], x_sb[:, 8 * c:8 * c + 8, :]).then_inc(s_st, 16)
            sp.wait_ge(s_st, 16 * CH)

        @block.tensor
        def _(pe):
            pe.wait_ge(s_load, 16 * n_loads)
            for i in range(NT // 2):
                for par in range(2):
                    t = 2 * i + par
                    pe.wait_ge(s_oT, t + 1)
                    for k in range(KD):
                        last = nc.tensor.transpose(m.psS[par][:, k * P:(k + 1) * P], m.gated[:, t, k * P:(k + 1) * P],
                                                   m.ident[:, :])
                    last.then_inc(s_tr, 1)
                    pe.wait_ge(s_oT, t + 3)
                    pe.wait_ge(s_free, t + 1)
                    for k in range(KD):
                        nc.tensor.matmul(m.psO[par][:, 0:D], oT[par][:, k, :], woT[:, k, :], start=k == 0, stop=False)
                    nc.tensor.matmul(m.psO[par][:, 0:D], m.ones_row[0:1, :], bo, start=False, stop=True)\
                        .then_inc(s_mm, 1)

        @block.scalar
        def _(act):
            act.sem_inc(s_oT, 2)
            act.sem_inc(s_mm, 1)
            act.wait_ge(s_y, 16)
            for c in range(CH):
                nc.scalar.activation(g_sb[:, 8 * c:8 * c + 8, :], g_sb[:, 8 * c:8 * c + 8, :], ACT.Silu)\
                    .then_inc(s_silu, 1)
            with act.Fori(0, NT // 2) as i:
                for par in range(2):
                    t = 2 * i + par
                    act.wait_ge(s_tr, t + 1)
                    act.wait_ge(s_mm, t + 1)
                    nc.scalar.activation(oT[par], m.psS[par][:, 0:D].rearrange("p (k t) -> p k t", k=KD), ACT.Copy)\
                        .then_inc(s_oT, 1)

        @block.vector
        def _(dve):
            dve.sem_inc(s_free, 2)
            dve.sem_inc(s_x, 1)
            dve.wait_ge(s_load, 16 * n_loads)
            dve.wait_ge(s_silu, CH)
            with dve.Fori(0, NT // 2) as i:
                for par in range(2):
                    t = 2 * i + par
                    dve.wait_ge(s_mm, t + 2)
                    dve.wait_ge(s_x, t + 1)
                    if L == 0:
                        nc.vector.tensor_tensor(tmp[par], m.psO[par][:, 0:D], xn_sb[:, t, :], ALU.add)\
                            .then_inc(s_free, 1)
                        dve.wait_ge(s_free, t + 3)
                        nc.vector.tensor_tensor(tmp[par], tmp[par], g_sb[:, t, :], ALU.mult).then_inc(s_sg, 1)
                    else:
                        nc.vector.tensor_tensor(tmp[par], m.psO[par][:, 0:D], g_sb[:, t, :], ALU.mult)\
                            .then_inc(s_free, 1)
                        dve.wait_ge(s_free, t + 3)
                    if L == 0:
                        dve.wait_ge(s_sg, t + 1)
                    nc.vector.tensor_tensor(x_sb[:, t, :], x_sb[:, t, :], tmp[par], ALU.add).then_inc(s_x, 1)


def program(nc, ins, out):
    with ExitStack() as ctx:
        m = Mem(nc, ctx)
        scratch = {
            "qk_parts": ((3, 2 * D, B * T), BF16), "norm_parts": ((3, 2 * HEADS, B * T), BF16),
            "xn_store": ((P, NT, D), F32), "xT_store": ((P, KD, B * T), F32), "y_store": ((NT, P, D), F32),
            "x1_store": ((B * T, D), F32),
        }
        io = dict(ins)
        io["out"] = out
        for name, (shape, dt) in scratch.items():
            io[name] = nc.dram_tensor(name, shape, dt, kind="Internal").ap()
        constants_phase(nc, m, io)
        for L in range(2):
            mine = dict(io)
            for name in ("wqk", "wvg", "woT", "bo"):
                mine[name] = io[f"{name}{L}"]
            weights_phase(nc, m, mine, L)
            norm_phase(nc, m, mine, L)
            projection_phase(nc, m, mine, L)
            attention_phase(nc, m, mine, L)
            output_phase(nc, m, mine, L)


def layout(inputs):
    import numpy as np

    a = {k: np.asarray(v) for k, v in inputs.items()}
    w_in = a["L0_attn_W_in"].reshape(HEADS, 4, DH, D)
    b_in = a["L0_attn_b_in"].reshape(HEADS, 4, DH)
    q, k, v, g = (w_in[:, i].reshape(D, D).T for i in range(4))
    bq, bk, bv, bg = (b_in[:, i].reshape(D) for i in range(4))
    sel = np.zeros((P, NQK, 2 * HEADS), np.float32)
    for f in range(NQK):
        for p in range(P):
            sel[p, f, f * (P // DH) + p // DH] = 1.0
    arrays = {
        "x": a["L0_attn_X"].reshape(B * T, D),
        "wqk0": np.concatenate([q, k], axis=1), "wvg0": np.concatenate([v, g], axis=1),
        "bqk": np.concatenate([bq, bk]).reshape(NQK, P).T, "bvg": np.concatenate([bv, bg]).reshape(1, 2 * D),
        "woT0": a["L0_attn_W_out"].T, "bo0": a["L0_attn_b_out"].reshape(1, D),
        "fast_bT": a["L0_ffn_fast_b"].T, "w_fc": a["L0_ffn_w_fc"], "w_proj": a["L0_ffn_w_proj"],
        "u_T": a["L0_ffn_u"].T, "v": a["L0_ffn_v"], "gate": a["L0_ffn_gate"].reshape(1, 1),
        "wqk1": np.concatenate([a["L1_attn_Wq"].T, a["L1_attn_Wk"].T], axis=1), "wvg1": a["L1_attn_Wv"].T,
        "woT1": a["L1_attn_Wo"].T, "bo1": a["L1_attn_bo"].reshape(1, D),
        "W1": a["L1_ffn_W1"], "b1": a["L1_ffn_b1"].reshape(FT, P), "W2": a["L1_ffn_W2"],
        "b2": a["L1_ffn_b2"].reshape(1, D),
        "ident": np.eye(P, dtype=np.float32), "sel": sel.reshape(P, NQK * 2 * HEADS),
        "selT": sel.transpose(2, 1, 0).reshape(2 * HEADS, NQK * P),
    }
    return {k: np.ascontiguousarray(v) for k, v in arrays.items()}


def kernel(**inputs):
    import concourse.bacc as bacc
    from concourse.bass_utils import run_bass_kernel_spmd

    nc = bacc.Bacc("TRN2", target_bir_lowering=False, num_devices=1)
    arrays = layout(inputs)
    ins = {k: nc.dram_tensor(f"in_{k}", v.shape, mybir.dt.from_np(v.dtype), kind="ExternalInput").ap()
           for k, v in arrays.items()}
    out = nc.dram_tensor("out", (B * T, D), F32, kind="ExternalOutput").ap()
    program(nc, ins, out)
    r = run_bass_kernel_spmd(nc, [{f"in_{k}": v for k, v in arrays.items()}], core_ids=[0])
    return r.results[0]["out"].reshape(B, T, D)
```

```python
import concourse.bass as bass
from concourse import mybir
from contextlib import ExitStack

F32 = mybir.dt.float32
BF16 = mybir.dt.bfloat16
ALU = mybir.AluOpType
ACT = mybir.ActivationFunctionType
X = mybir.AxisListType.X

B, T, D = 2, 2048, 256
HEADS = 16
DH = D // HEADS
HID = 4 * D
RANK = 16
P = 128
NT = B * T // P
KT = T // P
KD = D // P
FT = HID // P
QB = T // 512
TB = B * T // 512
NQK = 2 * D // P
VW = 32
LN_EPS = 1e-5
SHEP_EPS = 1e-4
NORM_EPS = 1e-6
SUM_EPS1 = 1e-6
COS_MAX = 0.999
PI = 3.141592653589793

PRODUCTS = [(0, 0), (0, 1), (0, 2), (1, 0), (1, 1), (2, 0)]
ROWS = DH * len(PRODUCTS)
NORM_ROWS = 6


class Mem:

    def __init__(self, nc, ctx):
        def sb(name, shape, dt=F32):
            return ctx.enter_context(nc.sbuf_tensor(name, shape, dt))

        self.w1T = sb("w1T", [P, KD, HID])
        self.w2T = sb("w2T", [P, FT, D])
        self.values = sb("values", [P, NT, D])
        self.gated = sb("gated", [P, NT, D])
        self.work = sb("work", [P, 3 * NT * D])
        self.q_stack = [sb(f"q_stack{b}", [P, T], BF16) for b in range(B)]
        self.k_stack = [sb(f"k_stack{b}", [P, T], BF16) for b in range(B)]
        self.v_tile = [sb(f"v_tile{b}", [P, KT, VW]) for b in range(B)]
        self.hidden = sb("hidden", [P, FT, P])
        self.ffn_in = sb("ffn_in", [P, KD, P])
        self.ffn_out = sb("ffn_out", [P, D])
        self.head_outT = sb("head_outT", [P, 512])
        self.ident = sb("ident", [P, P])
        self.ones_row = sb("ones_row", [1, P])
        self.b1_tiles = sb("b1_tiles", [FT, P])
        self.b2_row = sb("b2_row", [1, D])
        self.small = sb("small", [P, 8, NT])
        self.den = sb("den", [P, 2, KT])
        self.psS = [ctx.enter_context(nc.psum_tensor(f"psS{i}", [P, 1024], F32)) for i in range(2)]
        self.psO = [ctx.enter_context(nc.psum_tensor(f"psO{i}", [P, 512], F32)) for i in range(2)]
        self.psM = [ctx.enter_context(nc.psum_tensor(f"psM{i}", [P, 512], F32)) for i in range(2)]

    def area(self, start, *shape):
        n = 1
        for s in shape:
            n *= s
        flat = self.work[:, start:start + n]
        if len(shape) == 1:
            return flat
        names = "abc"[:len(shape)]
        return flat.rearrange(f"p ({' '.join(names)}) -> p {' '.join(names)}",
                              **{c: s for c, s in zip(names, shape)})


class Chain:

    def __init__(self, eng, sem):
        self.eng, self.sem, self.n = eng, sem, 0

    def __call__(self, ins):
        self.n += 1
        ins.then_inc(self.sem, 1)
        self.eng.wait_ge(self.sem, self.n)


def sems(nc, ctx, prefix, *names):
    made = [ctx.enter_context(nc.semaphore(f"{prefix}_{n}")) for n in names]
    ctx.callback(clear, nc, made)
    return made


def clear(nc, made):
    with nc.Block() as block:
        @block.sync
        def _(sp):
            for s in made:
                sp.sem_clear(s)


def constants_phase(nc, m, io):
    with ExitStack() as ctx:
        s_ident, s_set = sems(nc, ctx, "const", "ident", "set")
        block = ctx.enter_context(nc.Block())

        @block.sync
        def _(sp):
            sp.dma_start(m.ident[:, :], io["ident"]).then_inc(s_ident, 16)
            sp.wait_ge(s_ident, 16)

        @block.vector
        def _(dve):
            nc.vector.memset(m.ones_row[:, :], 1.0).then_inc(s_set, 1)
            for b in range(B):
                nc.vector.memset(m.v_tile[b][:, :, DH:DH + 1], 1.0).then_inc(s_set, 1)
                nc.vector.memset(m.v_tile[b][:, :, DH + 1:VW], 0.0).then_inc(s_set, 1)
                nc.vector.memset(m.q_stack[b][ROWS:P, :], 1.0).then_inc(s_set, 1)
                nc.vector.memset(m.k_stack[b][ROWS:P, :], 1.0).then_inc(s_set, 1)
            dve.wait_ge(s_set, 1 + 4 * B)


def weights_phase(nc, m, io, L):
    pre = f"w{L}"
    w1, w2 = (io["w_fc"], io["w_proj"]) if L == 0 else (io["W1"], io["W2"])
    BASE = NT * D
    raw1 = m.area(BASE, FT, D)
    raw2 = m.area(BASE + FT * D, KD, HID)
    mag = m.area(BASE + 2 * FT * D, FT, D)
    mag2 = m.area(BASE + 2 * FT * D, KD, HID)
    neg = m.area(BASE + 5 * FT * D, HID)
    u_T = m.area(BASE + 3 * FT * D + HID, HID)
    v_sb = m.area(BASE + 3 * FT * D + 2 * HID, D)
    fastT = m.area(BASE + 3 * FT * D + 2 * HID + D, RANK)
    gate = m.area(BASE + 3 * FT * D + 2 * HID + D + RANK, 1)
    gate_all = m.area(BASE + 3 * FT * D + 2 * HID + D + RANK + 1, 1)
    fv = m.area(BASE + 3 * FT * D + 2 * HID + 2 * D, D)
    ones = m.area(BASE + 3 * FT * D, P)
    S, HALF, NHALF = 0, 1, 2
    n_loads = 2 + (4 if L == 0 else 2)
    with ExitStack() as ctx:
        (s_x,) = sems(nc, ctx, pre, "x")
        s_load, s_dve, s_sum, s_rows, s_tern, s_tr, s_out, s_g, s_ga, s_fv, s_fvc, s_lr, s_add = sems(
            nc, ctx, pre, "load", "dve", "rows", "total", "tern", "transposed", "copied", "gate", "gate_copied",
            "fv", "fv_copied", "lowrank", "added")
        block = ctx.enter_context(nc.Block())

        @block.sync
        def _(sp):
            sp.dma_start(raw1, w1.rearrange("(f p) i -> p f i", p=P)).then_inc(s_load, 16)
            sp.dma_start(raw2, w2.rearrange("(k p) j -> p k j", p=P)).then_inc(s_load, 16)
            if L == 0:
                sp.dma_start(u_T[0:RANK, :], io["u_T"]).then_inc(s_load, 16)
                sp.dma_start(v_sb[0:RANK, :], io["v"]).then_inc(s_load, 16)
                sp.dma_start(fastT[0:RANK, :], io["fast_bT"]).then_inc(s_load, 16)
                sp.dma_start(gate[0:1, :], io["gate"]).then_inc(s_load, 16)
            else:
                sp.dma_start(m.b1_tiles[:, :], io["b1"]).then_inc(s_load, 16)
                sp.dma_start(m.b2_row[:, :], io["b2"]).then_inc(s_load, 16)
            if L == 0:
                sp.dma_start(m.area(0, NT, D), io["x"].rearrange("(t p) d -> p t d", p=P)).then_inc(s_x, 16)
                sp.wait_ge(s_x, 16)
            sp.wait_ge(s_load, 16 * n_loads)

        @block.vector
        def _(dve):
            link = Chain(dve, s_dve)
            if L == 1:
                link(nc.vector.memset(ones, 1.0))
            dve.wait_ge(s_load, 16 * n_loads)
            for i, (raw, mg, n, width) in enumerate(((raw1, mag, FT, D), (raw2, mag2, KD, HID))):
                c = slice(8 * i, 8 * i + n)
                link(nc.vector.scalar_tensor_tensor(mg, raw, -1.0, raw, ALU.mult, ALU.max))
                if L == 0:
                    link(nc.vector.tensor_reduce(m.small[:, S, c], mg, axis=X, op=ALU.add))
                    link(nc.vector.tensor_scalar(m.small[:, S, c], m.small[:, S, c], 1.0 / width, 1e-5,
                                                 ALU.mult, ALU.max))
                else:
                    nc.vector.tensor_reduce(m.small[:, 3, c], mg, axis=X, op=ALU.add).then_inc(s_sum, 1)
                    dve.wait_ge(s_rows, i + 1)
                    link(nc.vector.tensor_reduce(m.small[:, 4, i:i + 1], m.psM[i][:, 0:n], axis=X, op=ALU.add))
                    link(nc.vector.tensor_scalar(m.small[:, 5, i:i + 1], m.small[:, 4, i:i + 1],
                                                 1.0 / (D * HID), 1e-5, ALU.mult, ALU.add))
                    for j in range(n):
                        link(nc.vector.tensor_copy(m.small[:, S, 8 * i + j:8 * i + j + 1], m.small[:, 5, i:i + 1]))
                link(nc.vector.tensor_scalar(m.small[:, HALF, c], m.small[:, S, c], 0.5, None, ALU.mult))
                link(nc.vector.tensor_scalar(m.small[:, NHALF, c], m.small[:, S, c], -0.5, None, ALU.mult))
                for j in range(n):
                    a = slice(8 * i + j, 8 * i + j + 1)
                    link(nc.vector.tensor_scalar(neg[:, 0:width], raw[:, j, :], m.small[:, NHALF, a], None, ALU.is_lt))
                    link(nc.vector.scalar_tensor_tensor(raw[:, j, :], raw[:, j, :], m.small[:, HALF, a],
                                                        neg[:, 0:width], ALU.is_gt, ALU.subtract))
                    if L == 0:
                        link(nc.vector.tensor_scalar(raw[:, j, :], raw[:, j, :], m.small[:, S, a], None, ALU.mult))
            nc.vector.tensor_copy(m.small[:, 6, 0:1], m.small[:, S, 0:1]).then_inc(s_tern, 1)
            dve.wait_ge(s_tr, 1)
            for k in range(KD):
                nc.vector.tensor_copy(m.w1T[:, k, :], m.psS[k][:, :]).then_inc(s_out, 1)
            for j in range(4):
                ps = (m.psO + m.psM)[j]
                nc.vector.tensor_copy(m.w2T[:, 2 * j:2 * j + 2, :], ps[:, :].rearrange("p (a d) -> p a d", a=2))\
                    .then_inc(s_out, 1)
            if L == 0:
                dve.wait_ge(s_g, 1)
                nc.vector.tensor_copy(gate_all[0:RANK, :], m.psM[1][0:RANK, 0:1]).then_inc(s_ga, 1)
                dve.wait_ge(s_ga, 1)
                dve.wait_ge(s_fv, 1)
                nc.vector.tensor_scalar(fv[0:RANK, :], m.psM[0][0:RANK, 0:D], gate_all[0:RANK, :], None, ALU.mult)\
                    .then_inc(s_fvc, 1)
                for k in range(KD):
                    dve.wait_ge(s_lr, k + 1)
                    nc.vector.tensor_tensor(m.w1T[:, k, :], m.psS[k][:, :], m.w1T[:, k, :], ALU.add)\
                        .then_inc(s_add, 1)
                dve.wait_ge(s_add, KD)

        @block.tensor
        def _(pe):
            if L == 1:
                for i, n in enumerate((FT, KD)):
                    pe.wait_ge(s_sum, i + 1)
                    nc.tensor.matmul(m.psM[i][:, 0:n], ones, m.small[:, 3, 8 * i:8 * i + n],
                                     start=True, stop=True).then_inc(s_rows, 1)
            pe.wait_ge(s_tern, 1)
            for k in range(KD):
                for f in range(FT):
                    nc.tensor.transpose(m.psS[k][:, f * P:(f + 1) * P], raw1[:, f, k * P:(k + 1) * P], m.ident[:, :])
            for j in range(FT):
                ps = (m.psO + m.psM)[j // 2]
                for k in range(KD):
                    c = (j % 2) * D + k * P
                    last = nc.tensor.transpose(ps[:, c:c + P], raw2[:, k, j * P:(j + 1) * P], m.ident[:, :])
            last.then_inc(s_tr, 1)
            if L == 0:
                pe.wait_ge(s_out, 6)
                nc.tensor.matmul(m.psM[1][0:RANK, 0:1], m.ones_row[0:1, 0:RANK], gate[0:1, :], start=True, stop=True)\
                    .then_inc(s_g, 1)
                nc.tensor.matmul(m.psM[0][0:RANK, 0:D], fastT[0:RANK, :], v_sb[0:RANK, :], start=True, stop=True)\
                    .then_inc(s_fv, 1)
                pe.wait_ge(s_fvc, 1)
                for k in range(KD):
                    for c in range(2):
                        last = nc.tensor.matmul(m.psS[k][:, c * 512:(c + 1) * 512], fv[0:RANK, k * P:(k + 1) * P],
                                                u_T[0:RANK, c * 512:(c + 1) * 512], start=True, stop=True)
                    last.then_inc(s_lr, 1)


def norm_phase(nc, m, io, L):
    pre = f"n{L}"
    x_sb = m.area(0, NT, D)
    x2_sb = m.area(NT * D, NT, D)
    xTa = m.area(2 * NT * D, KD, B * T)
    xTf = m.values[:, :, :].rearrange("p a b -> p (a b)").rearrange("p (k t) -> p k t", k=KD)
    MEAN, VAR, RSTD, T0, T1 = 0, 1, 2, 3, 4
    UNROLL = 8
    GROUP = 4
    GROUPS = NT // GROUP
    stats = m.hidden[:, 0:2, :].rearrange("p a b -> p (a b)")[:, 0:NT * 6].rearrange("p (t s) -> p t s", s=6)
    norms = 2 if L == 0 else 1
    with ExitStack() as ctx:
        s_dve, s_var, s_std, s_tr, s_fr, s_st = sems(nc, ctx, pre, "dve", "var", "std", "transposed", "freed", "stored")
        s_norms = sems(nc, ctx, pre, "xn", "xn2")
        s_stats = sems(nc, ctx, pre, "stats1", "stats2")
        block = ctx.enter_context(nc.Block())

        @block.sync
        def _(sp):
            if L == 0:
                sp.wait_ge(s_norms[0], NT)
                sp.dma_start(io["xn_store"], x_sb).then_inc(s_st, 16)
                sp.wait_ge(s_fr, GROUPS)
                sp.dma_start(io["xT_store"], xTf).then_inc(s_st, 16)
                sp.wait_ge(s_st, 32)

        @block.vector
        def _(dve):
            link = Chain(dve, s_dve)
            for r in range(norms):
                src, dst = (x_sb, x_sb) if r == 0 else (x_sb, x2_sb)
                with dve.Fori(0, NT // UNROLL) as i:
                    for j in range(UNROLL):
                        t = UNROLL * i + j
                        nc.vector.bn_stats(stats[:, t, :], src[:, t, :]).then_inc(s_stats[r], 1)
                dve.wait_ge(s_stats[r], NT)
                st, sm = stats, m.small
                link(nc.vector.tensor_tensor(sm[:, MEAN, :], st[:, :, 1], st[:, :, 4], ALU.add))
                link(nc.vector.tensor_scalar(sm[:, MEAN, :], sm[:, MEAN, :], 0.5, None, ALU.mult))
                link(nc.vector.tensor_tensor(sm[:, T0, :], st[:, :, 1], st[:, :, 4], ALU.subtract))
                link(nc.vector.scalar_tensor_tensor(sm[:, T0, :], sm[:, T0, :], 0.25, sm[:, T0, :],
                                                    ALU.mult, ALU.mult))
                link(nc.vector.tensor_tensor(sm[:, T1, :], st[:, :, 2], st[:, :, 5], ALU.add))
                link(nc.vector.scalar_tensor_tensor(sm[:, VAR, :], sm[:, T1, :], 1.0 / D, sm[:, T0, :],
                                                    ALU.mult, ALU.add))
                nc.vector.tensor_scalar(sm[:, VAR, :], sm[:, VAR, :], LN_EPS, None, ALU.add).then_inc(s_var, 1)
                dve.wait_ge(s_std, r + 1)
                link(nc.vector.reciprocal(sm[:, RSTD, :], sm[:, T1, :]))
                with dve.Fori(0, NT // UNROLL) as i:
                    for j in range(UNROLL):
                        t = UNROLL * i + j
                        nc.vector.tensor_scalar(dst[:, t, :], src[:, t, :], sm[:, MEAN, bass.ds(t, 1)],
                                                sm[:, RSTD, bass.ds(t, 1)], ALU.subtract, ALU.mult)\
                            .then_inc(s_norms[r], 1)
                if r == 0 and norms == 2:
                    dve.wait_ge(s_norms[0], NT)

        @block.scalar
        def _(act):
            for r in range(norms):
                act.wait_ge(s_var, r + 1)
                nc.scalar.activation(m.small[:, T1, :], m.small[:, VAR, :], ACT.Sqrt).then_inc(s_std, 1)
                dst = xTf if r < norms - 1 else xTa
                for g in range(GROUPS):
                    act.wait_ge(s_tr, GROUPS * r + g + 1)
                    nc.scalar.activation(dst[:, :, g * GROUP * P:(g + 1) * GROUP * P],
                                         m.psS[g % 2][:, :].rearrange("p (k t) -> p k t", k=KD), ACT.Copy)\
                        .then_inc(s_fr, 1)

        @block.tensor
        def _(pe):
            for r in range(norms):
                src = x_sb if r == 0 else x2_sb
                for g in range(GROUPS):
                    pe.wait_ge(s_norms[r], GROUP * (g + 1))
                    if GROUPS * r + g >= 2:
                        pe.wait_ge(s_fr, GROUPS * r + g - 1)
                    for k in range(KD):
                        for t in range(GROUP):
                            c = (GROUP * k + t) * P
                            last = nc.tensor.transpose(m.psS[g % 2][:, c:c + P],
                                                       src[:, GROUP * g + t, k * P:(k + 1) * P], m.ident[:, :])
                    last.then_inc(s_tr, 1)


def split_parts(nc, link, src, parts, rest):
    link(nc.vector.tensor_copy(parts[:, 0, :], src))
    link(nc.vector.tensor_tensor(rest, src, parts[:, 0, :], ALU.subtract))
    link(nc.vector.tensor_copy(parts[:, 1, :], rest))
    return nc.vector.tensor_tensor(parts[:, 2, :], rest, parts[:, 1, :], ALU.subtract)


def projection_phase(nc, m, io, L):
    pre = f"p{L}"
    xTa = m.area(2 * NT * D, KD, B * T)
    vg_w = 2 * D if L == 0 else D
    wqk = m.area(0, KD, 2 * D)
    wvg = m.area(1024, KD, vg_w)
    bqk = m.area(2048, NQK)
    bvg = m.area(2052, 2 * D)
    bvg_all = m.area(2600, 2 * D)
    sel = m.area(3200, NQK, 2 * HEADS)
    selT = m.area(3400, NQK, P)
    projs = [m.area(at, NQK, 512) for at in (4096, 12288)]
    sq = m.area(6144, 2, 512)
    rest = m.area(7168, 512)
    parts = [m.work[:, 8192 + 768 * i:8192 + 768 * (i + 1)].bitcast(BF16).rearrange("p (a t) -> p a t", a=3)
             for i in range(2)]
    n_sb = m.area(9728, 512)
    n_rest = m.area(10240, 512)
    n_parts = m.work[:, 10752:11520].bitcast(BF16).rearrange("p (a t) -> p a t", a=3)
    r_norm = m.area(11520, 512)
    NR = 2 * HEADS
    n_loads = 6 if L == 0 else 4
    with ExitStack() as ctx:
        (s_load, s_dve, s_bias, s_bias_row, s_proj, s_P, s_sq, s_nm, s_nsb, s_nparts, s_nst, s_vps, s_vfree, s_rn,
         s_e, s_efree, s_parts, s_v) = sems(
            nc, ctx, pre, "load", "dve", "bias", "bias_rows", "proj", "projected", "squared", "norm_mm", "norm_copied",
            "norm_parts", "norm_stored", "v_ready", "v_free", "rnorm", "expanded", "expand_free", "parts",
            "values")
        s_st = sems(nc, ctx, pre, "stored0", "stored1")
        (s_xT,) = sems(nc, ctx, pre, "xT_stored")
        block = ctx.enter_context(nc.Block())

        @block.sync
        def _(sp):
            sp.dma_start(wqk, io["wqk"].rearrange("(k p) n -> p k n", p=P)).then_inc(s_load, 16)
            sp.dma_start(wvg, io["wvg"].rearrange("(k p) n -> p k n", p=P)).then_inc(s_load, 16)
            sp.dma_start(sel, io["sel"].rearrange("p (f r) -> p f r", f=NQK)).then_inc(s_load, 16)
            sp.dma_start(selT[0:NR], io["selT"].rearrange("p (f r) -> p f r", f=NQK)).then_inc(s_load, 16)
            if L == 0:
                sp.dma_start(bqk, io["bqk"]).then_inc(s_load, 16)
                sp.dma_start(bvg[0:1, :], io["bvg"]).then_inc(s_load, 16)
            if L == 1:
                sp.dma_start(io["xT_store"], xTa).then_inc(s_xT, 16)
            with sp.Fori(0, TB) as i:
                for ft in range(NQK):
                    sp.wait_ge(s_parts, 4 * i + ft + 9)
                    sp.dma_start(io["qk_parts"][:, ft * P:(ft + 1) * P, bass.ds(i * 512, 512)]
                                 .rearrange("a p t -> p a t"), parts[ft % 2]).then_inc(s_st[ft % 2], 16)
                if L == 0:
                    sp.wait_ge(s_nparts, i + 2)
                    sp.dma_start(io["norm_parts"][:, :, bass.ds(i * 512, 512)].rearrange("a p t -> p a t"),
                                 n_parts[0:NR]).then_inc(s_nst, 16)
            for x in s_st:
                sp.wait_ge(x, 16 * (2 * TB + 1))
            if L == 1:
                sp.wait_ge(s_xT, 16)
            if L == 0:
                sp.wait_ge(s_nst, 16 * (TB + 1))

        @block.tensor
        def _(pe):
            pe.sem_inc(s_nm, 2)
            pe.wait_ge(s_load, 16 * n_loads)
            if L == 0:
                nc.tensor.matmul(m.psM[0][:, :], m.ones_row[0:1, :], bvg[0:1, :], start=True, stop=True)\
                    .then_inc(s_bias_row, 1)
                pe.wait_ge(s_bias, 2)

            def norm(i, ft):
                pe.wait_ge(s_sq, 4 * i + ft + 1)
                if ft == 0:
                    pe.wait_ge(s_nsb, i + 1)
                nc.tensor.matmul(m.psO[0][0:NR, :], sel[:, ft, :], sq[:, ft % 2, :], start=ft == 0,
                                 stop=ft == NQK - 1).then_inc(s_nm, 1)

            def values(i, tts):
                for tt in tts:
                    pe.wait_ge(s_vfree, 4 * i + tt + 1)
                    for k in range(KD):
                        last = nc.tensor.matmul(m.psM[tt % 2][:, 0:vg_w], xTa[:, k, i * 512 + tt * P:i * 512 + (tt + 1) * P],
                                                wvg[:, k, :], start=k == 0, stop=k == KD - 1)
                    last.then_inc(s_vps, 1)

            def expand(i, ft):
                pe.wait_ge(s_rn, i + 2)
                pe.wait_ge(s_efree, 4 * i + ft + 1)
                nc.tensor.matmul(m.psS[ft % 2][:, 512:1024], selT[0:NR, ft, :], r_norm[0:NR, :], start=True, stop=True)\
                    .then_inc(s_e, 1)

            for i in range(TB):
                if L == 1:
                    values(i, range(4))
                for ft in range(NQK):
                    pe.wait_ge(s_P, 4 * i + ft + 1)
                    for k in range(KD):
                        last = nc.tensor.matmul(m.psS[ft % 2][:, 0:512], wqk[:, k, ft * P:(ft + 1) * P],
                                                xTa[:, k, i * 512:(i + 1) * 512], start=k == 0, stop=k == KD - 1)
                    last.then_inc(s_proj, 1)
                    if L == 0:
                        values(i, (ft,))
                    elif i > 0:
                        expand(i - 1, ft)
                    if ft > 0:
                        norm(i, ft - 1)
                norm(i, NQK - 1)
            if L == 1:
                for ft in range(NQK):
                    expand(TB - 1, ft)

        @block.scalar
        def _(act):
            act.sem_inc(s_P, 2)
            act.sem_inc(s_nsb, 1)
            if L == 0:
                act.wait_ge(s_bias, 2)
            def act_block(i, proj):
                if L == 1:
                    for tt in range(4):
                        act.wait_ge(s_vps, 4 * i + tt + 1)
                        nc.scalar.activation(m.values[:, bass.ds(4 * i + tt, 1), :], m.psM[tt % 2][:, 0:D].unsqueeze(1),
                                             ACT.Copy).then_inc(s_vfree, 1)
                for ft in range(NQK):
                    act.wait_ge(s_proj, 4 * i + ft + 1)
                    act.wait_ge(s_parts, 4 * i + ft + 1)
                    if L == 0:
                        nc.scalar.activation(proj[:, ft, :], m.psS[ft % 2][:, 0:512], ACT.Identity,
                                             bias=bqk[:, ft:ft + 1], scale=-2.0 if ft < 2 else 1.0).then_inc(s_P, 1)
                    else:
                        nc.scalar.activation(proj[:, ft, :], m.psS[ft % 2][:, 0:512], ACT.Copy).then_inc(s_P, 1)
                    act.wait_ge(s_P, 4 * i + ft + 3)
                    act.wait_ge(s_nm, 4 * i + ft + 1)
                    nc.scalar.activation(sq[:, ft % 2, :], proj[:, ft, :], ACT.Square,
                                         scale=0.5 if L == 0 and ft < 2 else 1.0).then_inc(s_sq, 1)
                act.wait_ge(s_nm, 4 * i + 6)
                if L == 0:
                    act.wait_ge(s_nparts, i + 1)
                else:
                    act.wait_ge(s_rn, i + 1)
                nc.scalar.activation(n_sb[0:NR, :], m.psO[0][0:NR, :], ACT.Copy if L == 0 else ACT.Sqrt)\
                    .then_inc(s_nsb, 1)

            with act.Fori(0, TB // 2) as ii:
                for par in range(2):
                    act_block(2 * ii + par, projs[par])

        @block.vector
        def _(dve):
            dve.sem_inc(s_parts, 8)
            dve.sem_inc(s_vfree, 2)
            dve.sem_inc(s_efree, 2)
            dve.sem_inc(s_nparts, 1)
            dve.sem_inc(s_rn, 1)
            for x in s_st + [s_nst]:
                dve.sem_inc(x, 16)
            per_block = NQK * 3 + (3 if L == 0 else 1)
            chain_n = [0]
            dve.wait_ge(s_load, 16 * n_loads)
            if L == 0:
                nc.vector.tensor_scalar(bqk[:, 0:2], bqk[:, 0:2], -2.0, None, ALU.mult).then_inc(s_bias, 1)
                dve.wait_ge(s_bias_row, 1)
                nc.vector.tensor_copy(bvg_all, m.psM[0][:, :]).then_inc(s_bias, 1)
                dve.wait_ge(s_bias, 2)
            def dve_block(i, proj):
                chain_n[0] = 0

                def link(ins):
                    chain_n[0] += 1
                    ins.then_inc(s_dve, 1)
                    dve.wait_ge(s_dve, per_block * i + chain_n[0])

                def split(ft):
                    dve.wait_ge(s_st[ft % 2], 32 * i + 16 * (ft // 2) + 16)
                    split_parts(nc, link, proj[:, ft, :], parts[ft % 2], rest).then_inc(s_parts, 1)
                    dve.wait_ge(s_parts, 4 * i + ft + 9)

                def value_tile(tt):
                    dve.wait_ge(s_vps, 4 * i + tt + 1)
                    t = 4 * i + tt
                    ps = m.psM[tt % 2]
                    nc.vector.tensor_tensor(m.values[:, t, :], ps[:, 0:D], bvg_all[:, 0:D], ALU.add)\
                        .then_inc(s_v, 1)
                    nc.vector.tensor_tensor(m.gated[:, t, :], ps[:, D:2 * D], bvg_all[:, D:2 * D], ALU.add)\
                        .then_inc(s_vfree, 1)

                if L == 0:
                    for ft in range(NQK):
                        dve.wait_ge(s_P, 4 * i + ft + 3)
                        split(ft)
                        value_tile(ft)
                    dve.wait_ge(s_nsb, i + 2)
                    dve.wait_ge(s_nst, 16 * i + 16)
                    split_parts(nc, link, n_sb[0:NR, :], n_parts[0:NR], n_rest[0:NR, :]).then_inc(s_nparts, 1)
                else:
                    dve.wait_ge(s_nsb, i + 2)
                    link(nc.vector.tensor_scalar(n_rest[0:NR, :], n_sb[0:NR, :], NORM_EPS, None, ALU.max))
                    nc.vector.reciprocal(r_norm[0:NR, :], n_rest[0:NR, :]).then_inc(s_rn, 1)
                    for ft in range(NQK):
                        dve.wait_ge(s_e, 4 * i + ft + 1)
                        nc.vector.tensor_tensor(proj[:, ft, :], m.psS[ft % 2][:, 512:1024], proj[:, ft, :], ALU.mult)\
                            .then_inc(s_efree, 1)
                        dve.wait_ge(s_efree, 4 * i + ft + 3)
                        split(ft)

            with dve.Fori(0, TB // 2) as ii:
                for par in range(2):
                    dve_block(2 * ii + par, projs[par])


def attention_phase(nc, m, io, L):
    pre = f"a{L}"
    UNITS = KT * B
    RING = 8
    ring = m.area(0, RING, T)
    q_ring = m.area(RING * T, 4, T)
    HALVES = (1, 0)
    LAG_PV = 5
    LAG_INV, LAG_SQ = 2, 3
    ACT_POW = 1664
    POW_STEPS = 5
    BATCH = 4
    ACT_SQ = 1024
    rows = ROWS + NORM_ROWS if L == 0 else ROWS
    loads = 2 * len(PRODUCTS) + (2 if L == 0 else 0)
    values = m.values[:, :, :].rearrange("p (b k) (h d) -> p b k h d", b=B, h=HEADS)
    gated = m.gated[:, :, :].rearrange("p (b q a) (h d) -> p b q a h d", b=B, q=QB, h=HEADS)
    EPS_SUM = SHEP_EPS if L == 0 else SUM_EPS1
    with ExitStack() as ctx:
        (s_qk, s_pv, s_fin, s_h, s_r, s_yps, s_yo, s_yst, s_o, s_ot, s_den, s_rec, s_g, s_vt) = sems(
            nc, ctx, pre, "scores", "pv", "ffn_loaded", "ffn_hidden", "ffn_relu", "ffn_sum", "ffn_copied",
            "ffn_stored", "out_copied", "out_transposed", "den", "rec", "gated", "v_tile")
        if L == 0:
            s_a, s_y, s_m, s_v, s_wa, s_wd, s_r2, s_g0 = sems(
                nc, ctx, pre, "inv_dist", "quot", "guarded", "inv_shifted", "w_act", "w_dve", "ffn_squared", "gated0")
        else:
            s_cl, s_q, s_rs, s_ls, s_z, s_at, s_ln, s_w, s_pw = sems(
                nc, ctx, pre, "clipped", "cos2", "rsin", "log_sin", "tan_half", "angle", "log", "w_act", "w_dve")
        s_stk = sems(nc, ctx, pre, "stack0", "stack1")
        block = ctx.enter_context(nc.Block())

        def pairs(eng, body):
            body(0, True, False)
            with eng.Fori(1, HEADS - 1) as h:
                body(h, False, False)
            body(HEADS - 1, False, True)

        @block.sync
        def _(sp):
            def head(h, first, last):
                for b in range(B):
                    if not first:
                        sp.wait_ge(s_qk, 2 * (UNITS * h + KT * b + KT - UNITS))
                    tok = slice(b * T, (b + 1) * T)
                    for side, stack in ((0, m.q_stack[b]), (1, m.k_stack[b])):
                        for g, pr in enumerate(PRODUCTS):
                            sp.dma_start(stack[g * DH:(g + 1) * DH, :],
                                         io["qk_parts"][pr[side], bass.ds(h * DH + side * D, DH), tok])\
                                .then_inc(s_stk[b], 16)
                        if L == 0:
                            at = ROWS + 3 * side
                            sp.dma_start(stack[at:at + 3, :],
                                         io["norm_parts"][:, bass.ds(h + HEADS * side, 1), tok]
                                         .rearrange("a o t -> (a o) t")).then_inc(s_stk[b], 16)
                    if not (first and b == 0):
                        sp.wait_ge(s_h, 2 * (2 * h + b))
                    sp.dma_start(m.ffn_in[:, :, :], io["xT_store"][:, :, bass.ds((2 * h + b) * P, P)])\
                        .then_inc(s_fin, 16)
            pairs(sp, head)

        @block.gpsimd
        def _(pool):
            def head(h, first, last):
                for b in range(B):
                    if not first:
                        pool.wait_ge(s_pv, UNITS * h + KT * b + KT - UNITS)
                    nc.gpsimd.tensor_copy(m.v_tile[b][:, :, 0:DH], values[:, b, :, h, :]).then_inc(s_vt, 1)
            pairs(pool, head)

        def pe_scores(pe, h, u, first, halves=(0, 1)):
            b, kt = u // KT, u % KT
            if kt == 0 and halves[0] == 0:
                pe.wait_ge(s_stk[b], 16 * loads * (h + 1))
            for half in halves:
                if not (first and u == 0):
                    pe.wait_ge(s_y if L == 0 else s_cl, 2 * (UNITS * h + u) + half - 1)
                for q in range(2):
                    c = (2 * half + q) * 512
                    last = nc.tensor.matmul(m.psS[half][:, q * 512:(q + 1) * 512],
                                            m.k_stack[b][0:rows, kt * P:(kt + 1) * P],
                                            m.q_stack[b][0:rows, c:c + 512], start=True, stop=True)
                last.then_inc(s_qk, 1)

        def pe_values(pe, h, u, first, blocks=range(QB)):
            n = UNITS * h + u
            b, kt = (u % UNITS) // KT, u % KT
            if blocks[0] == 0:
                if kt == 0:
                    pe.wait_ge(s_vt, 2 * h + (u // KT) + 1)
                    if not (first and 0 <= u < UNITS):
                        pe.wait_ge(s_o, 2 * h + (u // KT) - 1)
                if L == 0:
                    pe.wait_ge(s_wa, n + 1)
                    pe.wait_ge(s_wd, n + 1)
                else:
                    pe.wait_ge(s_w, n + 1)
                    pe.wait_ge(s_pw, POW_STEPS * (UNITS // BATCH * h + u // BATCH + 1))
            for q in blocks:
                last = nc.tensor.matmul(m.psO[b][VW * q:VW * (q + 1), :], m.v_tile[b][:, kt, :],
                                        ring[:, u % RING, q * 512:(q + 1) * 512], start=kt == 0, stop=kt == KT - 1)
            if blocks[-1] == QB - 1:
                last.then_inc(s_pv, 1)

        def pe_out(pe, n):
            pe.wait_ge(s_o, n + 1)
            for a in range(4):
                last = nc.tensor.transpose(m.psM[1][:, a * P:(a + 1) * P], m.head_outT[:, a * P:(a + 1) * P],
                                           m.ident[:, :])
            last.then_inc(s_ot, 1)

        def pe_hidden(pe, n, quarters=range(4)):
            for quarter in quarters:
                if quarter == 0:
                    pe.wait_ge(s_fin, 16 * (n + 1))
                g = HALVES[quarter // 2]
                for f in range(2 * (quarter % 2), 2 * (quarter % 2) + 2):
                    for k in range(KD):
                        c = (4 * g + f) * P
                        last = nc.tensor.matmul(m.psM[g][:, f * P:(f + 1) * P], m.w1T[:, k, c:c + P],
                                                m.ffn_in[:, k, :], start=k == 0 and (L == 0 or f == 0),
                                                stop=L == 0 and k == KD - 1)
                if quarter % 2 == 0:
                    continue
                if L == 1:
                    last = nc.tensor.matmul(m.psM[g][:, :], m.b1_tiles[:, :],
                                            m.ident[0:FT, 4 * g:4 * g + 4].unsqueeze(2).broadcast_to([FT, 4, P]),
                                            start=False, stop=True)
                last.then_inc(s_h, 1)

        def pe_ffn_sum(pe, n, fs=range(FT)):
            if fs[0] == 0:
                pe.wait_ge(s_r if L == 1 else s_r2, 2 * (n + 1))
            for f in fs:
                last = nc.tensor.matmul(m.psM[0][:, 0:D], m.hidden[:, f, :], m.w2T[:, f, :], start=f == 0,
                                        stop=L == 0 and f == FT - 1)
            if L == 1:
                last = nc.tensor.matmul(m.psM[0][:, 0:D], m.ones_row[0:1, :], m.b2_row[0:1, :], start=False, stop=True)
            if fs[-1] == FT - 1:
                last.then_inc(s_yps, 1)

        def act_out(act, n, b):
            act.wait_ge(s_pv, KT * (n + 1))
            act.wait_ge(s_ot, n)
            nc.scalar.activation(m.head_outT[:, :], m.psO[b][:, :], ACT.Copy).then_inc(s_o, 1)

        def act_relu(act, n, order=range(2)):
            act.wait_ge(s_yps, n)
            for i in order:
                g = HALVES[i]
                act.wait_ge(s_h, 2 * n + i + 1)
                nc.scalar.activation(m.hidden[:, 4 * g:4 * g + 4, :], m.psM[g][:, :].rearrange("p (f t) -> p f t", f=4),
                                     ACT.Relu).then_inc(s_r, 1)

        def act_ffn_out(act, n):
            act.wait_ge(s_yps, n + 1)
            act.wait_ge(s_yst, 16 * n)
            nc.scalar.activation(m.ffn_out[:, :], m.psM[0][:, 0:D], ACT.Copy).then_inc(s_yo, 1)
            act.wait_ge(s_yo, n + 1)
            act.dma_start(io["y_store"][bass.ds(n, 1), :, :].rearrange("o p d -> (o p) d"), m.ffn_out[:, :])\
                .then_inc(s_yst, 16)

        def dve_out(dve, h, b, n):
            dve.wait_ge(s_ot, n + 1)
            ps = m.psM[1][:, :].rearrange("p (a q c) -> p q a c", a=4, q=QB)
            den = m.den[:, 0, :].rearrange("p (q a) -> p q a", q=QB)
            rec = m.den[:, 1, :].rearrange("p (q a) -> p q a", q=QB)
            nc.vector.tensor_scalar(den, ps[:, :, :, DH], EPS_SUM, None, ALU.add).then_inc(s_den, 1)
            dve.wait_ge(s_den, n + 1)
            nc.vector.reciprocal(m.den[:, 1, :], m.den[:, 0, :]).then_inc(s_rec, 1)
            dve.wait_ge(s_rec, n + 1)
            out = gated[:, b, :, :, h, :]
            rec16 = rec.unsqueeze(3).broadcast_to([P, QB, 4, DH])
            if L == 0:
                nc.vector.tensor_tensor(out, ps[:, :, :, 0:DH], out, ALU.mult).then_inc(s_g0, 1)
                dve.wait_ge(s_g0, n + 1)
                nc.vector.tensor_tensor(out, out, rec16, ALU.mult).then_inc(s_g, 1)
            else:
                nc.vector.tensor_tensor(out, ps[:, :, :, 0:DH], rec16, ALU.mult).then_inc(s_g, 1)

        if L == 0:
            OUT_COPY, OUT_T, OUT_DIV = 5, 7, 8
            HID = (0, 1, 2, 3)
            RELU, SQ = (2, 4), (4, 6)
            SUM = {8: (0,), 9: (1,), 10: (2,), 11: (3,), 12: (4,), 13: (5,), 14: (6, 7)}
            COPY = 15

            @block.tensor
            def _(pe):
                def head(h, first, last):
                    for u in range(UNITS + (LAG_PV if last else 0)):
                        b, kt = u // KT, u % KT
                        n = 2 * h + b
                        if u < UNITS:
                            pe_scores(pe, h, u, first, (0,))
                        if not (first and u < LAG_PV):
                            pe_values(pe, h, u - LAG_PV, first)
                        if u < UNITS:
                            pe_scores(pe, h, u, first, (1,))
                        if kt == 0 and not first:
                            pe.wait_ge(s_g, n - 1)
                        if kt == 2 and not (first and b == 0):
                            pe.wait_ge(s_yo, n)
                        if kt in HID and u < UNITS:
                            pe_hidden(pe, n, (HID.index(kt),))
                        if kt == OUT_T and u < UNITS and not (first and b == 0):
                            pe.wait_ge(s_r, 2 * n + 1)
                            pe_out(pe, n - 1)
                        if kt in SUM:
                            pe_ffn_sum(pe, n, SUM[kt])
                    if last:
                        pe_out(pe, 2 * HEADS - 1)
                pairs(pe, head)

            @block.scalar
            def _(act):
                def head(h, first, last):
                    def inverse_distance(u, half):
                        c = UNITS * h + u
                        if half == 0 and not (first and u < RING):
                            act.wait_ge(s_pv, c - RING + 1)
                        act.wait_ge(s_qk, 2 * c + half + 1)
                        nc.scalar.activation(ring[:, u % RING, half * 1024:(half + 1) * 1024],
                                             m.psS[half][:, :], ACT.Abs_reciprocal_sqrt).then_inc(s_a, 1)

                    for u in range(UNITS + (LAG_SQ if last else 0)):
                        b, kt = u // KT, u % KT
                        n = 2 * h + b
                        c = UNITS * h + u
                        if u < UNITS:
                            inverse_distance(u, 0)
                        if u < UNITS + LAG_INV and not (first and u < LAG_INV):
                            act.wait_ge(s_m, c - LAG_INV + 1)
                            slot = ring[:, (u - LAG_INV) % RING, :]
                            nc.scalar.activation(slot, slot, ACT.Abs_reciprocal_sqrt, bias=SHEP_EPS * SHEP_EPS,
                                                 scale=2 * SHEP_EPS).then_inc(s_v, 1)
                        if u < UNITS:
                            inverse_distance(u, 1)
                        if not (first and u < LAG_SQ):
                            act.wait_ge(s_v, c - LAG_SQ + 1)
                            slot = ring[:, (u - LAG_SQ) % RING, 0:ACT_SQ]
                            nc.scalar.activation(slot, slot, ACT.Square).then_inc(s_wa, 1)
                        if kt == OUT_COPY and not (first and b == 0) and u < UNITS:
                            act_out(act, n - 1, (b + 1) % 2)
                        if kt in RELU and u < UNITS:
                            act_relu(act, n, (RELU.index(kt),))
                        if kt == COPY:
                            act_ffn_out(act, n)
                    if last:
                        act_out(act, 2 * HEADS - 1, 1)
                        act.wait_ge(s_yst, 16 * 2 * HEADS)
                pairs(act, head)

            @block.vector
            def _(dve):
                def head(h, first, last):
                    def quotient(u, half):
                        c = UNITS * h + u
                        dve.wait_ge(s_a, 2 * c + half + 1)
                        part = ring[:, u % RING, half * 1024:(half + 1) * 1024]
                        nc.vector.scalar_tensor_tensor(part, part, 0.5 / SHEP_EPS, m.psS[half][:, :],
                                                       ALU.add, ALU.mult).then_inc(s_y, 1)

                    for u in range(UNITS + (LAG_SQ if last else 0)):
                        b, kt = u // KT, u % KT
                        n = 2 * h + b
                        c = UNITS * h + u
                        if u < UNITS:
                            quotient(u, 0)
                        if u <= UNITS and not (first and u < 1):
                            dve.wait_ge(s_y, 2 * c)
                            slot = ring[:, (u - 1) % RING, :]
                            nc.vector.tensor_scalar(slot, slot, 0.0, None, ALU.max).then_inc(s_m, 1)
                        if u < UNITS:
                            quotient(u, 1)
                        if not (first and u < LAG_SQ):
                            dve.wait_ge(s_v, c - LAG_SQ + 1)
                            part = ring[:, (u - LAG_SQ) % RING, ACT_SQ:T]
                            nc.vector.tensor_tensor(part, part, part, ALU.mult).then_inc(s_wd, 1)
                        if kt == OUT_DIV and not (first and b == 0) and u < UNITS:
                            dve_out(dve, h if b else h - 1, 1 - b, n - 1)
                        if kt in SQ:
                            g = HALVES[SQ.index(kt)]
                            dve.wait_ge(s_r, 2 * n + SQ.index(kt) + 1)
                            part = m.hidden[:, 4 * g:4 * g + 4, :]
                            nc.vector.tensor_tensor(part, part, part, ALU.mult).then_inc(s_r2, 1)
                    if last:
                        dve_out(dve, HEADS - 1, 1, 2 * HEADS - 1)
                pairs(dve, head)
        else:
            NB = UNITS // BATCH

            @block.tensor
            def _(pe):
                def head(h, first, last):
                    for j in range(NB + (1 if last else 0)):
                        n = 2 * h + j // 4
                        if first and j == 0:
                            pe_scores(pe, h, 0, True)
                        for u in range(BATCH * j + 1, min(BATCH * (j + 1) + 1, UNITS)):
                            pe_scores(pe, h, u, first)
                        if j == NB - 1 and not last:
                            pe_scores(pe, h + 1, 0, False)
                        if not (first and j == 0):
                            for u in range(BATCH * (j - 1), BATCH * j):
                                pe_values(pe, h, u, first)
                        if j % 4 == 1 and not (first and j < 4):
                            pe_out(pe, n - 1)
                        if j % 4 == 2:
                            if not (first and j < 4):
                                pe.wait_ge(s_yo, n)
                                pe.wait_ge(s_g, n)
                            pe_hidden(pe, n)
                        if j % 4 == 3:
                            pe_ffn_sum(pe, n)
                    if last:
                        pe_out(pe, 2 * HEADS - 1)
                pairs(pe, head)

            @block.scalar
            def _(act):
                def head(h, first, last):
                    for j in range(NB):
                        n = 2 * h + j // 4
                        twos = [(BATCH * j + 2 * i, BATCH * j + 2 * i + 1) for i in range(BATCH // 2)]
                        if j == 0:
                            nc.scalar.preload_act_table_set("natural_log_exp_and_others")
                        for u, v in twos:
                            act.wait_ge(s_q, UNITS * h + v + 1)
                            pair = q_ring[:, u % BATCH:u % BATCH + 2, :]
                            nc.scalar.activation(pair, pair, ACT.Ln, bias=1.0, scale=-1.0).then_inc(s_ls, 1)
                        for u in range(BATCH * j, BATCH * (j + 1)):
                            act.wait_ge(s_ls, UNITS // 2 * h + u // 2 + 1)
                            slot = q_ring[:, u % BATCH, :]
                            nc.scalar.activation(slot, slot, ACT.Sigmoid, scale=-0.5).then_inc(s_rs, 1)
                        for u, v in twos:
                            act.wait_ge(s_z, UNITS * h + v + 1)
                            pair = ring[:, u % RING:u % RING + 2, :]
                            nc.scalar.activation(pair, pair, ACT.Arctan).then_inc(s_at, 1)
                        nc.scalar.preload_act_table_set("natural_log_exp_and_others")
                        for u, v in twos:
                            act.wait_ge(s_at, UNITS // 2 * h + u // 2 + 1)
                            pair = ring[:, u % RING:u % RING + 2, 0:ACT_POW]
                            nc.scalar.activation(pair, pair, ACT.Ln, bias=0.5, scale=2.0 / PI)\
                                .then_inc(s_ln, 1)
                        for u, v in twos:
                            act.wait_ge(s_ln, UNITS // 2 * h + u // 2 + 1)
                            pair = ring[:, u % RING:u % RING + 2, 0:ACT_POW]
                            nc.scalar.activation(pair, pair, ACT.Exp, scale=16.0).then_inc(s_w, 2)
                        if j % 4 == 0 and not (first and j == 0):
                            act_out(act, n - 1, (j // 4 + 1) % 2)
                        if j % 4 == 2:
                            act_relu(act, n)
                        if j % 4 == 3:
                            act_ffn_out(act, n)
                    if last:
                        act_out(act, 2 * HEADS - 1, 1)
                        act.wait_ge(s_yst, 16 * 2 * HEADS)
                pairs(act, head)

            @block.vector
            def _(dve):
                def head(h, first, last):
                    def cosines(u):
                        c = UNITS * h + u
                        if not (first and u < RING):
                            dve.wait_ge(s_pv, c - RING + 1)
                        for half in range(2):
                            dve.wait_ge(s_qk, 2 * c + half + 1)
                            nc.vector.tensor_scalar(ring[:, u % RING, half * 1024:(half + 1) * 1024],
                                                    m.psS[half][:, :], COS_MAX, -COS_MAX, ALU.min, ALU.max)\
                                .then_inc(s_cl, 1)

                    def square_cosines(u):
                        c = UNITS * h + u
                        dve.wait_ge(s_cl, 2 * c + 2)
                        nc.vector.tensor_tensor(q_ring[:, u % BATCH, :], ring[:, u % RING, :], ring[:, u % RING, :],
                                                ALU.mult).then_inc(s_q, 1)

                    def powers(j):
                        dve.wait_ge(s_at, UNITS // 2 * h + 2 * j + 2)
                        first_slot = (BATCH * j) % RING
                        part = ring[:, first_slot:first_slot + BATCH, ACT_POW:T]
                        done = POW_STEPS * (NB * h + j)
                        nc.vector.tensor_scalar(part, part, 2.0 / PI, 0.5, ALU.mult, ALU.add).then_inc(s_pw, 1)
                        for i in range(1, POW_STEPS):
                            dve.wait_ge(s_pw, done + i)
                            nc.vector.tensor_tensor(part, part, part, ALU.mult).then_inc(s_pw, 1)

                    for j in range(NB + (1 if last else 0)):
                        n = 2 * h + j // 4
                        us = range(BATCH * j, BATCH * (j + 1))
                        if j < NB:
                            cosines(us[0])
                            cosines(us[1])
                            square_cosines(us[0])
                            square_cosines(us[1])
                            cosines(us[2])
                            cosines(us[3])
                            square_cosines(us[2])
                            square_cosines(us[3])
                        if not (first and j == 0):
                            powers(j - 1)
                        if j < NB:
                            for u in us:
                                dve.wait_ge(s_rs, UNITS * h + u + 1)
                                slot = ring[:, u % RING, :]
                                nc.vector.tensor_tensor(slot, slot, q_ring[:, u % BATCH, :], ALU.mult).then_inc(s_z, 1)
                            dve.wait_ge(s_z, UNITS * h + BATCH * (j + 1))
                        if j < NB and j % 4 == 1 and not (first and j < 4):
                            dve_out(dve, h if j >= 4 else h - 1, (j // 4 + 1) % 2, n - 1)
                    if last:
                        dve_out(dve, HEADS - 1, 1, 2 * HEADS - 1)
                pairs(dve, head)


def output_phase(nc, m, io, L):
    pre = f"o{L}"
    x_sb = m.area(0, NT, D)
    xn_sb = m.area(NT * D, NT, D)
    g_sb = m.area(2 * NT * D, NT, D)
    woT = m.hidden[:, 0:4, :].rearrange("p (k a) b -> p k (a b)", k=KD)
    bo = m.ffn_out[0:1, :]
    oT = [m.w1T[:, i, 0:2 * D].rearrange("p (a k t) -> p a k t", a=2, k=KD) for i in range(2)]
    tmp = [m.w2T[:, 2 * i:2 * i + 2, :] for i in range(2)]
    CH = 4
    PAIRS = NT // 2
    CP = PAIRS // CH
    with ExitStack() as ctx:
        s_w, s_silu, s_tr, s_oT, s_mm, s_free, s_sg, s_x, s_st = sems(
            nc, ctx, pre, "weights", "silu", "transposed", "copied", "product", "free", "sg", "x", "stored")
        s_load = sems(nc, ctx, pre, *[f"load{c}" for c in range(CH)])
        block = ctx.enter_context(nc.Block())
        n_loads = 3 if L == 0 else 2
        x_view = (io["x"] if L == 0 else io["x1_store"]).rearrange("(t p) d -> p t d", p=P)
        out_view = (io["x1_store"] if L == 0 else io["out"]).rearrange("(t p) d -> p t d", p=P)

        def pair(buf, n):
            return buf[:, bass.ds(2 * n, 2), :]

        @block.sync
        def _(sp):
            sp.dma_start(woT, io["woT"].rearrange("(k p) n -> p k n", p=P)).then_inc(s_w, 16)
            sp.dma_start(bo, io["bo"]).then_inc(s_w, 16)
            for c in range(CH):
                t = slice(2 * CP * c, 2 * CP * (c + 1))
                sp.dma_start(g_sb[:, t, :], io["y_store"].rearrange("t p d -> p t d")[:, t, :]).then_inc(s_load[c], 16)
                if L == 0:
                    sp.dma_start(xn_sb[:, t, :], io["xn_store"][:, t, :]).then_inc(s_load[c], 16)
                sp.dma_start(x_sb[:, t, :], x_view[:, t, :]).then_inc(s_load[c], 16)
            for c in range(CH):
                t = slice(2 * CP * c, 2 * CP * (c + 1))
                sp.wait_ge(s_x, CP * (c + 1))
                sp.dma_start(out_view[:, t, :], x_sb[:, t, :]).then_inc(s_st, 16)
            sp.wait_ge(s_st, 16 * CH)

        @block.tensor
        def _(pe):
            def transposes(n):
                if n >= 2:
                    pe.wait_ge(s_oT, n - 1)
                for a in range(2):
                    for k in range(KD):
                        c = (KD * a + k) * P
                        last = nc.tensor.transpose(m.psS[n % 2][:, c:c + P], m.gated[:, 2 * n + a, k * P:(k + 1) * P],
                                                   m.ident[:, :])
                last.then_inc(s_tr, 1)

            transposes(0)
            pe.wait_ge(s_w, 32)
            for n in range(PAIRS):
                if n + 1 < PAIRS:
                    transposes(n + 1)
                if n >= 2:
                    pe.wait_ge(s_free, n - 1)
                nc.tensor.matmul(m.psO[n % 2][:, :], m.ones_row[0:1, :], bo.unsqueeze(1).broadcast_to([1, 2, D]),
                                 start=True, stop=False)
                pe.wait_ge(s_oT, n + 1)
                for a in range(2):
                    for k in range(KD):
                        last = nc.tensor.matmul(m.psO[n % 2][:, a * D:(a + 1) * D], oT[n % 2][:, a, k, :],
                                                woT[:, k, :], start=False, stop=a == 1 and k == KD - 1)
                last.then_inc(s_mm, 1)

        @block.scalar
        def _(act):
            act.sem_inc(s_mm, 1)
            for c in range(CH):
                act.wait_ge(s_load[c], 16 * n_loads)
                g = g_sb[:, 2 * CP * c:2 * CP * (c + 1), :]
                nc.scalar.activation(g, g, ACT.Silu).then_inc(s_silu, 1)
                with act.Fori(0, CP // 2) as i:
                    for par in range(2):
                        n = CP * c + 2 * i + par
                        act.wait_ge(s_tr, n + 1)
                        act.wait_ge(s_mm, n + 1)
                        nc.scalar.activation(oT[par], m.psS[par][:, 0:2 * D]
                                             .rearrange("p (a k t) -> p a k t", a=2, k=KD), ACT.Copy).then_inc(s_oT, 1)

        @block.vector
        def _(dve):
            for c in range(CH):
                dve.wait_ge(s_silu, c + 1)
                dve.wait_ge(s_load[c], 16 * n_loads)
                with dve.Fori(0, CP // 2) as i:
                    for par in range(2):
                        n = CP * c + 2 * i + par
                        dve.wait_ge(s_mm, n + 2)
                        ps = m.psO[par][:, :].rearrange("p (a d) -> p a d", a=2)
                        if L == 0:
                            nc.vector.tensor_tensor(tmp[par], ps, pair(xn_sb, n), ALU.add).then_inc(s_free, 1)
                            dve.wait_ge(s_free, n + 1)
                            nc.vector.tensor_tensor(tmp[par], tmp[par], pair(g_sb, n), ALU.mult).then_inc(s_sg, 1)
                            dve.wait_ge(s_sg, n + 1)
                        else:
                            nc.vector.tensor_tensor(tmp[par], ps, pair(g_sb, n), ALU.mult).then_inc(s_free, 1)
                            dve.wait_ge(s_free, n + 1)
                        nc.vector.tensor_tensor(pair(x_sb, n), pair(x_sb, n), tmp[par], ALU.add).then_inc(s_x, 1)


def program(nc, ins, out):
    with ExitStack() as ctx:
        m = Mem(nc, ctx)
        scratch = {
            "qk_parts": ((3, 2 * D, B * T), BF16), "norm_parts": ((3, 2 * HEADS, B * T), BF16),
            "xn_store": ((P, NT, D), F32), "xT_store": ((P, KD, B * T), F32), "y_store": ((NT, P, D), F32),
            "x1_store": ((B * T, D), F32),
        }
        io = dict(ins)
        io["out"] = out
        for name, (shape, dt) in scratch.items():
            io[name] = nc.dram_tensor(name, shape, dt, kind="Internal").ap()
        constants_phase(nc, m, io)
        for L in range(2):
            mine = dict(io)
            for name in ("wqk", "wvg", "woT", "bo"):
                mine[name] = io[f"{name}{L}"]
            weights_phase(nc, m, mine, L)
            norm_phase(nc, m, mine, L)
            projection_phase(nc, m, mine, L)
            attention_phase(nc, m, mine, L)
            output_phase(nc, m, mine, L)


def layout(inputs):
    import numpy as np

    a = {k: np.asarray(v) for k, v in inputs.items()}
    w_in = a["L0_attn_W_in"].reshape(HEADS, 4, DH, D)
    b_in = a["L0_attn_b_in"].reshape(HEADS, 4, DH)
    q, k, v, g = (w_in[:, i].reshape(D, D).T for i in range(4))
    bq, bk, bv, bg = (b_in[:, i].reshape(D) for i in range(4))
    sel = np.zeros((P, NQK, 2 * HEADS), np.float32)
    for f in range(NQK):
        for p in range(P):
            sel[p, f, f * (P // DH) + p // DH] = 1.0
    arrays = {
        "x": a["L0_attn_X"].reshape(B * T, D),
        "wqk0": np.concatenate([q, k], axis=1), "wvg0": np.concatenate([v, g], axis=1),
        "bqk": np.concatenate([bq, bk]).reshape(NQK, P).T, "bvg": np.concatenate([bv, bg]).reshape(1, 2 * D),
        "woT0": a["L0_attn_W_out"].T, "bo0": a["L0_attn_b_out"].reshape(1, D),
        "fast_bT": a["L0_ffn_fast_b"].T, "w_fc": a["L0_ffn_w_fc"], "w_proj": a["L0_ffn_w_proj"],
        "u_T": a["L0_ffn_u"].T, "v": a["L0_ffn_v"], "gate": a["L0_ffn_gate"].reshape(1, 1),
        "wqk1": np.concatenate([a["L1_attn_Wq"].T, a["L1_attn_Wk"].T], axis=1), "wvg1": a["L1_attn_Wv"].T,
        "woT1": a["L1_attn_Wo"].T, "bo1": a["L1_attn_bo"].reshape(1, D),
        "W1": a["L1_ffn_W1"], "b1": a["L1_ffn_b1"].reshape(FT, P), "W2": a["L1_ffn_W2"],
        "b2": a["L1_ffn_b2"].reshape(1, D),
        "ident": np.eye(P, dtype=np.float32), "sel": sel.reshape(P, NQK * 2 * HEADS),
        "selT": sel.transpose(2, 1, 0).reshape(2 * HEADS, NQK * P),
    }
    return {k: np.ascontiguousarray(v) for k, v in arrays.items()}


def kernel(**inputs):
    import concourse.bacc as bacc
    from concourse.bass_utils import run_bass_kernel_spmd

    nc = bacc.Bacc("TRN2", target_bir_lowering=False, num_devices=1)
    arrays = layout(inputs)
    ins = {k: nc.dram_tensor(f"in_{k}", v.shape, mybir.dt.from_np(v.dtype), kind="ExternalInput").ap()
           for k, v in arrays.items()}
    out = nc.dram_tensor("out", (B * T, D), F32, kind="ExternalOutput").ap()
    program(nc, ins, out)
    r = run_bass_kernel_spmd(nc, [{f"in_{k}": v for k, v in arrays.items()}], core_ids=[0])
    return r.results[0]["out"].reshape(B, T, D)
```

```python
import concourse.bass as bass
from concourse import mybir
from contextlib import ExitStack

F32 = mybir.dt.float32
BF16 = mybir.dt.bfloat16
ALU = mybir.AluOpType
ACT = mybir.ActivationFunctionType
X = mybir.AxisListType.X

B, T, D = 2, 2048, 256
HEADS = 16
DH = D // HEADS
HID = 4 * D
RANK = 16
P = 128
NT = B * T // P
KT = T // P
KD = D // P
FT = HID // P
QB = T // 512
TB = B * T // 512
NQK = 2 * D // P
FH = P // DH
NCOL = 32
VW = 32
LN_EPS = 1e-5
SHEP_EPS = 1e-4
NORM_EPS = 1e-6
ZERO_SHIFT = 1e-24
SUM_EPS1 = 1e-6
COS_MAX = 0.999
PI = 3.141592653589793

PRODUCTS = [(0, 0), (0, 1), (0, 2), (1, 0), (1, 1), (2, 0)]
ROWS = DH * len(PRODUCTS)
NORM_ROWS = 6


class Mem:

    def __init__(self, nc, ctx):
        def sb(name, shape, dt=F32):
            return ctx.enter_context(nc.sbuf_tensor(name, shape, dt))

        self.w1T = sb("w1T", [P, KD, HID])
        self.w2T = sb("w2T", [P, FT, D])
        self.values = sb("values", [P, NT, D])
        self.gated = sb("gated", [P, NT, D])
        self.work = sb("work", [P, 3 * NT * D])
        self.q_stack = [sb(f"q_stack{b}", [P, T], BF16) for b in range(B)]
        self.k_stack = [sb(f"k_stack{b}", [P, T], BF16) for b in range(B)]
        self.v_tile = [sb(f"v_tile{b}", [P, KT, VW]) for b in range(B)]
        self.hidden = sb("hidden", [P, FT, P])
        self.ffn_in = sb("ffn_in", [P, KD, P])
        self.ffn_out = sb("ffn_out", [P, D])
        self.head_outT = sb("head_outT", [P, 512])
        self.ident = sb("ident", [P, P])
        self.ones_row = sb("ones_row", [1, P])
        self.b1_tiles = sb("b1_tiles", [FT, P])
        self.b2_row = sb("b2_row", [1, D])
        self.small = sb("small", [P, 8, NT])
        self.den = sb("den", [P, 2, KT])
        self.psS = [ctx.enter_context(nc.psum_tensor(f"psS{i}", [P, 1024], F32)) for i in range(2)]
        self.psO = [ctx.enter_context(nc.psum_tensor(f"psO{i}", [P, 512], F32)) for i in range(2)]
        self.psM = [ctx.enter_context(nc.psum_tensor(f"psM{i}", [P, 512], F32)) for i in range(2)]

    def area(self, start, *shape):
        n = 1
        for s in shape:
            n *= s
        flat = self.work[:, start:start + n]
        if len(shape) == 1:
            return flat
        names = "abc"[:len(shape)]
        return flat.rearrange(f"p ({' '.join(names)}) -> p {' '.join(names)}",
                              **{c: s for c, s in zip(names, shape)})


class Chain:

    def __init__(self, eng, sem):
        self.eng, self.sem, self.n = eng, sem, 0

    def __call__(self, ins):
        self.n += 1
        ins.then_inc(self.sem, 1)
        self.eng.wait_ge(self.sem, self.n)


def sems(nc, ctx, prefix, *names):
    made = [ctx.enter_context(nc.semaphore(f"{prefix}_{n}")) for n in names]
    ctx.callback(clear, nc, made)
    return made


def clear(nc, made):
    with nc.Block() as block:
        @block.sync
        def _(sp):
            for s in made:
                sp.sem_clear(s)


def raw_weights(m):
    flat = m.values[:, :, :].rearrange("p a b -> p (a b)")
    n = FT * D
    return (flat[:, 0:n].rearrange("p (f i) -> p f i", f=FT), flat[:, n:2 * n].rearrange("p (k j) -> p k j", k=KD))


def lowrank_factors(m):
    at = 2 * NT * D
    return {"u_T": m.area(at, HID)[0:RANK], "v": m.area(at + HID, D)[0:RANK],
            "fast_bT": m.area(at + HID + D, RANK)[0:RANK], "gate": m.area(at + HID + D + RANK, 1)[0:1]}


def load_weights(sp, m, io, L, loaded):
    w1, w2 = (io["w_fc"], io["w_proj"]) if L == 0 else (io["W1"], io["W2"])
    raw1, raw2 = raw_weights(m)
    sp.dma_start(raw1, w1.rearrange("(f p) i -> p f i", p=P)).then_inc(loaded, 16)
    sp.dma_start(raw2, w2.rearrange("(k p) j -> p k j", p=P)).then_inc(loaded, 16)
    if L == 0:
        small = [(buf, io[name]) for name, buf in lowrank_factors(m).items()]
    else:
        small = [(m.b1_tiles[:, :], io["b1"]), (m.b2_row[:, :], io["b2"])]
    for buf, src in small:
        sp.dma_start(buf, src).then_inc(loaded, 16)
    return 16 * (2 + len(small))


def constants_phase(nc, m, io):
    with ExitStack() as ctx:
        s_ident, s_set, s_w = sems(nc, ctx, "const", "ident", "set", "weights")
        block = ctx.enter_context(nc.Block())

        @block.sync
        def _(sp):
            loads = load_weights(sp, m, io, 0, s_w)
            sp.dma_start(m.ident[:, :], io["ident"]).then_inc(s_ident, 16)
            sp.wait_ge(s_ident, 16)
            sp.wait_ge(s_w, loads)

        @block.vector
        def _(dve):
            nc.vector.memset(m.ones_row[:, :], 1.0).then_inc(s_set, 1)
            for b in range(B):
                nc.vector.memset(m.v_tile[b][:, :, DH:DH + 1], 1.0).then_inc(s_set, 1)
                nc.vector.memset(m.v_tile[b][:, :, DH + 1:VW], 0.0).then_inc(s_set, 1)
                nc.vector.memset(m.q_stack[b][ROWS:P, :], 1.0).then_inc(s_set, 1)
                nc.vector.memset(m.k_stack[b][ROWS:P, :], 1.0).then_inc(s_set, 1)
            dve.wait_ge(s_set, 1 + 4 * B)


def weights_phase(nc, m, io, L):
    pre = f"w{L}"
    BASE = NT * D
    raws = raw_weights(m)
    mags = (m.area(BASE, FT, D), m.area(BASE + FT * D, KD, HID))
    tiles, widths = (FT, KD), (D, HID)
    ones = m.area(BASE + 2 * FT * D, P)
    gate_all = m.area(BASE + 2 * FT * D + P, 1)
    fv = m.area(BASE + 2 * FT * D + 2 * P, D)
    small = lowrank_factors(m)
    S, HALF, NHALF, ROW, TOTAL = 0, 1, 2, 3, 4
    NS = FT + KD
    with ExitStack() as ctx:
        (s_x, s_abs, s_dve, s_sum, s_rows, s_lt, s_sign, s_tern, s_tr, s_w1, s_w2, s_g, s_ga, s_fv, s_fvc, s_lr,
         s_add) = sems(
            nc, ctx, pre, "x", "abs", "dve", "rows", "total", "below", "sign", "tern", "transposed", "w1_copied",
            "w2_copied", "gate", "gate_copied", "fv", "fv_copied", "lowrank", "added")
        block = ctx.enter_context(nc.Block())

        @block.sync
        def _(sp):
            if L == 0:
                sp.dma_start(m.area(0, NT, D), io["x"].rearrange("(t p) d -> p t d", p=P)).then_inc(s_x, 16)
                sp.wait_ge(s_x, 16)

        @block.vector
        def _(dve):
            link = Chain(dve, s_dve)
            sm = m.small
            if L == 1:
                link(nc.vector.memset(ones, 1.0))
            link(nc.vector.scalar_tensor_tensor(mags[0], raws[0], -1.0, raws[0], ALU.mult, ALU.max))
            nc.vector.tensor_reduce(sm[:, ROW, 0:FT], mags[0], axis=X, op=ALU.add).then_inc(s_sum, 1)
            dve.wait_ge(s_abs, 1)
            nc.vector.tensor_reduce(sm[:, ROW, FT:NS], mags[1], axis=X, op=ALU.add).then_inc(s_sum, 1)
            dve.wait_ge(s_sum, 2)
            if L == 0:
                used = NS
                link(nc.vector.tensor_scalar(sm[:, S, 0:FT], sm[:, ROW, 0:FT], 1.0 / D, 1e-5, ALU.mult, ALU.max))
                link(nc.vector.tensor_scalar(sm[:, S, FT:NS], sm[:, ROW, FT:NS], 1.0 / HID, 1e-5, ALU.mult, ALU.max))
            else:
                used = 2
                dve.wait_ge(s_rows, 1)
                link(nc.vector.tensor_reduce(sm[:, TOTAL, 0:1], m.psM[0][:, 0:FT], axis=X, op=ALU.add))
                link(nc.vector.tensor_reduce(sm[:, TOTAL, 1:2], m.psM[0][:, FT:NS], axis=X, op=ALU.add))
                link(nc.vector.tensor_scalar(sm[:, S, 0:2], sm[:, TOTAL, 0:2], 1.0 / (D * HID), 1e-5,
                                             ALU.mult, ALU.add))
            link(nc.vector.tensor_scalar(sm[:, HALF, 0:used], sm[:, S, 0:used], 0.5, None, ALU.mult))
            link(nc.vector.tensor_scalar(sm[:, NHALF, 0:used], sm[:, S, 0:used], -0.5, None, ALU.mult))
            below, sign = s_lt, (s_sign if L == 0 else s_tern)
            done = 0
            for i in range(2):
                cuts = [(slice(j, j + 1), FT * i + j) for j in range(tiles[i])] if L == 0 else [(slice(None), i)]
                for cut, a in cuts:
                    nc.vector.tensor_scalar(mags[i][:, cut, :], raws[i][:, cut, :], sm[:, NHALF, a:a + 1], None,
                                            ALU.is_lt).then_inc(below, 1)
                for cut, a in cuts:
                    done += 1
                    dve.wait_ge(below, done)
                    nc.vector.scalar_tensor_tensor(raws[i][:, cut, :], raws[i][:, cut, :], sm[:, HALF, a:a + 1],
                                                   mags[i][:, cut, :], ALU.is_gt, ALU.subtract).then_inc(sign, 1)
            dve.wait_ge(s_tr, 2)
            for j in range(4):
                ps = (m.psO + m.psM)[j]
                nc.vector.tensor_copy(m.w2T[:, 2 * j:2 * j + 2, :], ps[:, :].rearrange("p (a d) -> p a d", a=2))\
                    .then_inc(s_w2, 1)
            if L == 0:
                dve.wait_ge(s_g, 1)
                nc.vector.tensor_copy(gate_all[0:RANK, :], m.psM[1][0:RANK, 0:1]).then_inc(s_ga, 1)
                dve.wait_ge(s_ga, 1)
                dve.wait_ge(s_fv, 1)
                nc.vector.tensor_scalar(fv[0:RANK, :], m.psM[0][0:RANK, 0:D], gate_all[0:RANK, :], None, ALU.mult)\
                    .then_inc(s_fvc, 1)
                dve.wait_ge(s_w1, KD)
                for k in range(KD):
                    dve.wait_ge(s_lr, k + 1)
                    nc.vector.tensor_tensor(m.w1T[:, k, :], m.psS[k][:, :], m.w1T[:, k, :], ALU.add)\
                        .then_inc(s_add, 1)
                dve.wait_ge(s_add, KD)

        @block.scalar
        def _(act):
            nc.scalar.activation(mags[1], raws[1], ACT.Abs).then_inc(s_abs, 1)
            if L == 0:
                for i in range(2):
                    for j in range(tiles[i]):
                        a = FT * i + j
                        act.wait_ge(s_sign, a + 1)
                        nc.scalar.activation(raws[i][:, j, :], raws[i][:, j, :], ACT.Copy,
                                             scale=m.small[:, S, a:a + 1]).then_inc(s_tern, 1)
            act.wait_ge(s_tr, 1)
            for k in range(KD):
                nc.scalar.activation(m.w1T[:, k, :], m.psS[k][:, :], ACT.Copy).then_inc(s_w1, 1)

        @block.tensor
        def _(pe):
            if L == 1:
                pe.wait_ge(s_sum, 2)
                nc.tensor.matmul(m.psM[0][:, 0:NS], ones, m.small[:, 3, 0:NS], start=True, stop=True)\
                    .then_inc(s_rows, 1)
            pe.wait_ge(s_tern, FT if L == 0 else 1)
            for k in range(KD):
                for f in range(FT):
                    last = nc.tensor.transpose(m.psS[k][:, f * P:(f + 1) * P], raws[0][:, f, k * P:(k + 1) * P],
                                               m.ident[:, :])
            last.then_inc(s_tr, 1)
            pe.wait_ge(s_tern, NS if L == 0 else 2)
            for j in range(FT):
                ps = (m.psO + m.psM)[j // 2]
                for k in range(KD):
                    c = (j % 2) * D + k * P
                    last = nc.tensor.transpose(ps[:, c:c + P], raws[1][:, k, j * P:(j + 1) * P], m.ident[:, :])
            last.then_inc(s_tr, 1)
            if L == 0:
                pe.wait_ge(s_w1, KD)
                pe.wait_ge(s_w2, 4)
                nc.tensor.matmul(m.psM[1][0:RANK, 0:1], m.ones_row[0:1, 0:RANK], small["gate"], start=True, stop=True)\
                    .then_inc(s_g, 1)
                nc.tensor.matmul(m.psM[0][0:RANK, 0:D], small["fast_bT"], small["v"], start=True, stop=True)\
                    .then_inc(s_fv, 1)
                pe.wait_ge(s_fvc, 1)
                for k in range(KD):
                    for c in range(2):
                        last = nc.tensor.matmul(m.psS[k][:, c * 512:(c + 1) * 512], fv[0:RANK, k * P:(k + 1) * P],
                                                small["u_T"][:, c * 512:(c + 1) * 512], start=True, stop=True)
                    last.then_inc(s_lr, 1)


def norm_phase(nc, m, io, L):
    pre = f"n{L}"
    x_sb = m.area(0, NT, D)
    x2_sb = m.area(NT * D, NT, D)
    xTa = m.area(2 * NT * D, KD, B * T)
    xTf = m.values[:, :, :].rearrange("p a b -> p (a b)").rearrange("p (k t) -> p k t", k=KD)
    MEAN, VAR, RSTD, T0, T1 = 0, 1, 2, 3, 4
    UNROLL = 8
    GROUP = 4
    GROUPS = NT // GROUP
    stats = m.hidden[:, 0:2, :].rearrange("p a b -> p (a b)")[:, 0:NT * 6].rearrange("p (t s) -> p t s", s=6)
    norms = 2 if L == 0 else 1
    with ExitStack() as ctx:
        s_dve, s_var, s_std, s_tr, s_fr, s_st = sems(nc, ctx, pre, "dve", "var", "std", "transposed", "freed", "stored")
        s_norms = sems(nc, ctx, pre, "xn", "xn2")
        s_stats = sems(nc, ctx, pre, "stats1", "stats2")
        block = ctx.enter_context(nc.Block())

        @block.sync
        def _(sp):
            if L == 0:
                sp.wait_ge(s_norms[0], NT)
                sp.dma_start(io["xn_store"], x_sb).then_inc(s_st, 16)
                sp.wait_ge(s_fr, GROUPS)
                sp.dma_start(io["xT_store"], xTf).then_inc(s_st, 16)
                sp.wait_ge(s_st, 32)

        @block.vector
        def _(dve):
            link = Chain(dve, s_dve)
            for r in range(norms):
                src, dst = (x_sb, x_sb) if r == 0 else (x_sb, x2_sb)
                with dve.Fori(0, NT // UNROLL) as i:
                    for j in range(UNROLL):
                        t = UNROLL * i + j
                        nc.vector.bn_stats(stats[:, t, :], src[:, t, :]).then_inc(s_stats[r], 1)
                dve.wait_ge(s_stats[r], NT)
                st, sm = stats, m.small
                link(nc.vector.tensor_tensor(sm[:, MEAN, :], st[:, :, 1], st[:, :, 4], ALU.add))
                link(nc.vector.tensor_scalar(sm[:, MEAN, :], sm[:, MEAN, :], 0.5, None, ALU.mult))
                link(nc.vector.tensor_tensor(sm[:, T0, :], st[:, :, 1], st[:, :, 4], ALU.subtract))
                link(nc.vector.scalar_tensor_tensor(sm[:, T0, :], sm[:, T0, :], 0.25, sm[:, T0, :],
                                                    ALU.mult, ALU.mult))
                link(nc.vector.tensor_tensor(sm[:, T1, :], st[:, :, 2], st[:, :, 5], ALU.add))
                link(nc.vector.scalar_tensor_tensor(sm[:, VAR, :], sm[:, T1, :], 1.0 / D, sm[:, T0, :],
                                                    ALU.mult, ALU.add))
                nc.vector.tensor_scalar(sm[:, VAR, :], sm[:, VAR, :], LN_EPS, None, ALU.add).then_inc(s_var, 1)
                dve.wait_ge(s_std, r + 1)
                link(nc.vector.reciprocal(sm[:, RSTD, :], sm[:, T1, :]))
                with dve.Fori(0, NT // UNROLL) as i:
                    for j in range(UNROLL):
                        t = UNROLL * i + j
                        nc.vector.tensor_scalar(dst[:, t, :], src[:, t, :], sm[:, MEAN, bass.ds(t, 1)],
                                                sm[:, RSTD, bass.ds(t, 1)], ALU.subtract, ALU.mult)\
                            .then_inc(s_norms[r], 1)
                if r == 0 and norms == 2:
                    dve.wait_ge(s_norms[0], NT)

        @block.scalar
        def _(act):
            for r in range(norms):
                act.wait_ge(s_var, r + 1)
                nc.scalar.activation(m.small[:, T1, :], m.small[:, VAR, :], ACT.Sqrt).then_inc(s_std, 1)
                dst = xTf if r < norms - 1 else xTa
                for g in range(GROUPS):
                    act.wait_ge(s_tr, GROUPS * r + g + 1)
                    nc.scalar.activation(dst[:, :, g * GROUP * P:(g + 1) * GROUP * P],
                                         m.psS[g % 2][:, :].rearrange("p (k t) -> p k t", k=KD), ACT.Copy)\
                        .then_inc(s_fr, 1)

        @block.tensor
        def _(pe):
            for r in range(norms):
                src = x_sb if r == 0 else x2_sb
                for g in range(GROUPS):
                    pe.wait_ge(s_norms[r], GROUP * (g + 1))
                    if GROUPS * r + g >= 2:
                        pe.wait_ge(s_fr, GROUPS * r + g - 1)
                    for k in range(KD):
                        for t in range(GROUP):
                            c = (GROUP * k + t) * P
                            last = nc.tensor.transpose(m.psS[g % 2][:, c:c + P],
                                                       src[:, GROUP * g + t, k * P:(k + 1) * P], m.ident[:, :])
                    last.then_inc(s_tr, 1)


def split_parts(nc, link, src, parts, rest):
    link(nc.vector.tensor_copy(parts[:, 0, :], src))
    link(nc.vector.tensor_tensor(rest, src, parts[:, 0, :], ALU.subtract))
    link(nc.vector.tensor_copy(parts[:, 1, :], rest))
    return nc.vector.tensor_tensor(parts[:, 2, :], rest, parts[:, 1, :], ALU.subtract)


def projection_phase(nc, m, io, L):
    pre = f"p{L}"
    xTa = m.area(2 * NT * D, KD, B * T)
    vg_w = 2 * D if L == 0 else D
    wqk = m.area(0, KD, 2 * D)
    wvg = m.area(1024, KD, vg_w)
    bqk = m.area(2048, NQK)
    bvg = m.area(2052, 2 * D)
    bvg_all = m.area(2600, 2 * D)
    sel = m.area(3200, NCOL)
    selT = m.area(3400, P)
    projs = [m.area(at, NQK, 512) for at in (4096, 12288)]
    sq = m.area(14336, NQK, 512)
    rest = m.area(7168, 512)
    parts = [m.work[:, 8192 + 768 * i:8192 + 768 * (i + 1)].bitcast(BF16).rearrange("p (a t) -> p a t", a=3)
             for i in range(2)]
    n_sb = m.area(9728, 512)
    n_rest = m.area(10240, 512)
    n_parts = m.work[:, 10752:11520].bitcast(BF16).rearrange("p (a t) -> p a t", a=3)
    r_norm = m.area(11520, 512)
    n_loads = 6 if L == 0 else 4
    with ExitStack() as ctx:
        (s_load, s_dve, s_bias, s_bias_row, s_proj, s_P, s_sq, s_nm, s_nsb, s_nparts, s_nst, s_vps, s_vfree, s_rn,
         s_e, s_efree, s_parts, s_v) = sems(
            nc, ctx, pre, "load", "dve", "bias", "bias_rows", "proj", "projected", "squared", "norm_mm", "norm_copied",
            "norm_parts", "norm_stored", "v_ready", "v_free", "rnorm", "expanded", "expand_free", "parts",
            "values")
        s_st = sems(nc, ctx, pre, "stored0", "stored1")
        (s_xT,) = sems(nc, ctx, pre, "xT_stored")
        block = ctx.enter_context(nc.Block())

        @block.sync
        def _(sp):
            sp.dma_start(wqk, io["wqk"].rearrange("(k p) n -> p k n", p=P)).then_inc(s_load, 16)
            sp.dma_start(wvg, io["wvg"].rearrange("(k p) n -> p k n", p=P)).then_inc(s_load, 16)
            sp.dma_start(sel, io["sel"]).then_inc(s_load, 16)
            sp.dma_start(selT, io["selT"]).then_inc(s_load, 16)
            if L == 0:
                sp.dma_start(bqk, io["bqk"]).then_inc(s_load, 16)
                sp.dma_start(bvg[0:1, :], io["bvg"]).then_inc(s_load, 16)
            if L == 1:
                sp.dma_start(io["xT_store"], xTa).then_inc(s_xT, 16)
            with sp.Fori(0, TB) as i:
                for ft in range(NQK):
                    sp.wait_ge(s_parts, 4 * i + ft + 9)
                    sp.dma_start(io["qk_parts"][:, ft * P:(ft + 1) * P, bass.ds(i * 512, 512)]
                                 .rearrange("a p t -> p a t"), parts[ft % 2]).then_inc(s_st[ft % 2], 16)
                if L == 0:
                    sp.wait_ge(s_nparts, i + 2)
                    for f in range(NQK):
                        sp.dma_start(io["norm_parts"][:, f * FH:(f + 1) * FH, bass.ds(i * 512, 512)]
                                     .rearrange("a p t -> p a t"), n_parts[f * NCOL:f * NCOL + FH]).then_inc(s_nst, 16)
            for x in s_st:
                sp.wait_ge(x, 16 * (2 * TB + 1))
            if L == 1:
                sp.wait_ge(s_xT, 16)
            if L == 0:
                sp.wait_ge(s_nst, 16 * (NQK * TB + 1))

        @block.tensor
        def _(pe):
            pe.sem_inc(s_nm, 1)
            pe.wait_ge(s_load, 16 * n_loads)
            if L == 0:
                nc.tensor.matmul(m.psM[0][:, :], m.ones_row[0:1, :], bvg[0:1, :], start=True, stop=True)\
                    .then_inc(s_bias_row, 1)
                pe.wait_ge(s_bias, 2)

            def norms(i):
                pe.wait_ge(s_sq, NQK * (i + 1))
                pe.wait_ge(s_nsb, i + 1)
                for f in range(NQK):
                    last = nc.tensor.matmul(m.psO[0][f * NCOL:(f + 1) * NCOL, :], sel, sq[:, f, :],
                                            start=True, stop=True)
                last.then_inc(s_nm, 1)

            def values(i, tts):
                for tt in tts:
                    pe.wait_ge(s_vfree, 4 * i + tt + 1)
                    for k in range(KD):
                        last = nc.tensor.matmul(m.psM[tt % 2][:, 0:vg_w], xTa[:, k, i * 512 + tt * P:i * 512 + (tt + 1) * P],
                                                wvg[:, k, :], start=k == 0, stop=k == KD - 1)
                    last.then_inc(s_vps, 1)

            def expand(i, ft):
                pe.wait_ge(s_rn, i + 2)
                pe.wait_ge(s_efree, 4 * i + ft + 1)
                rows = slice(ft * NCOL, (ft + 1) * NCOL)
                nc.tensor.matmul(m.psS[ft % 2][:, 512:1024], selT[rows, :], r_norm[rows, :], start=True, stop=True)\
                    .then_inc(s_e, 1)

            for i in range(TB):
                if L == 1:
                    values(i, range(2))
                for ft in range(NQK):
                    pe.wait_ge(s_P, 4 * i + ft + 1)
                    for k in range(KD):
                        last = nc.tensor.matmul(m.psS[ft % 2][:, 0:512], wqk[:, k, ft * P:(ft + 1) * P],
                                                xTa[:, k, i * 512:(i + 1) * 512], start=k == 0, stop=k == KD - 1)
                    last.then_inc(s_proj, 1)
                    if L == 0:
                        values(i, (ft,))
                    elif i > 0:
                        expand(i - 1, ft)
                if L == 1:
                    values(i, (2, 3))
                norms(i)
            if L == 1:
                for ft in range(NQK):
                    expand(TB - 1, ft)

        @block.scalar
        def _(act):
            act.sem_inc(s_P, 2)
            act.sem_inc(s_nsb, 1)
            if L == 0:
                act.wait_ge(s_bias, 2)
            def act_block(i, proj):
                def value_tile(tt):
                    act.wait_ge(s_vps, 4 * i + tt + 1)
                    nc.scalar.activation(m.values[:, bass.ds(4 * i + tt, 1), :], m.psM[tt % 2][:, 0:D].unsqueeze(1),
                                         ACT.Copy).then_inc(s_vfree, 1)

                if L == 1:
                    for tt in range(2):
                        value_tile(tt)
                act.wait_ge(s_nm, i + 1)
                for ft in range(NQK):
                    act.wait_ge(s_proj, 4 * i + ft + 1)
                    act.wait_ge(s_parts, 4 * i + ft + 1)
                    if L == 0:
                        nc.scalar.activation(proj[:, ft, :], m.psS[ft % 2][:, 0:512], ACT.Identity,
                                             bias=bqk[:, ft:ft + 1], scale=-2.0 if ft < 2 else 1.0).then_inc(s_P, 1)
                    else:
                        nc.scalar.activation(proj[:, ft, :], m.psS[ft % 2][:, 0:512], ACT.Copy).then_inc(s_P, 1)
                    act.wait_ge(s_P, 4 * i + ft + 3)
                    nc.scalar.activation(sq[:, ft, :], proj[:, ft, :], ACT.Square,
                                         scale=0.5 if L == 0 and ft < 2 else 1.0).then_inc(s_sq, 1)
                if L == 1:
                    value_tile(2)
                    value_tile(3)
                act.wait_ge(s_nm, i + 2)
                if L == 0:
                    act.wait_ge(s_nparts, i + 1)
                else:
                    act.wait_ge(s_rn, i + 1)
                if L == 0:
                    nc.scalar.activation(n_sb, m.psO[0][:, :], ACT.Copy).then_inc(s_nsb, 1)
                else:
                    nc.scalar.activation(n_sb, m.psO[0][:, :], ACT.Abs_reciprocal_sqrt, bias=ZERO_SHIFT)\
                        .then_inc(s_nsb, 1)

            with act.Fori(0, TB // 2) as ii:
                for par in range(2):
                    act_block(2 * ii + par, projs[par])

        @block.vector
        def _(dve):
            dve.sem_inc(s_parts, 8)
            dve.sem_inc(s_vfree, 2)
            dve.sem_inc(s_efree, 2)
            dve.sem_inc(s_nparts, 1)
            dve.sem_inc(s_rn, 1)
            for x in s_st + [s_nst]:
                dve.sem_inc(x, 16)
            per_block = NQK * 3 + (3 if L == 0 else 0)
            chain_n = [0]
            dve.wait_ge(s_load, 16 * n_loads)
            if L == 0:
                nc.vector.tensor_scalar(bqk[:, 0:2], bqk[:, 0:2], -2.0, None, ALU.mult).then_inc(s_bias, 1)
                dve.wait_ge(s_bias_row, 1)
                nc.vector.tensor_copy(bvg_all, m.psM[0][:, :]).then_inc(s_bias, 1)
                dve.wait_ge(s_bias, 2)
            def dve_block(i, proj):
                chain_n[0] = 0

                def link(ins):
                    chain_n[0] += 1
                    ins.then_inc(s_dve, 1)
                    dve.wait_ge(s_dve, per_block * i + chain_n[0])

                def split(ft):
                    dve.wait_ge(s_st[ft % 2], 32 * i + 16 * (ft // 2) + 16)
                    split_parts(nc, link, proj[:, ft, :], parts[ft % 2], rest).then_inc(s_parts, 1)
                    dve.wait_ge(s_parts, 4 * i + ft + 9)

                def value_tile(tt):
                    dve.wait_ge(s_vps, 4 * i + tt + 1)
                    t = 4 * i + tt
                    ps = m.psM[tt % 2]
                    nc.vector.tensor_tensor(m.values[:, t, :], ps[:, 0:D], bvg_all[:, 0:D], ALU.add)\
                        .then_inc(s_v, 1)
                    nc.vector.tensor_tensor(m.gated[:, t, :], ps[:, D:2 * D], bvg_all[:, D:2 * D], ALU.add)\
                        .then_inc(s_vfree, 1)

                if L == 0:
                    for ft in range(NQK):
                        dve.wait_ge(s_P, 4 * i + ft + 3)
                        split(ft)
                        value_tile(ft)
                    dve.wait_ge(s_nsb, i + 2)
                    dve.wait_ge(s_nst, 16 * NQK * i + 16)
                    split_parts(nc, link, n_sb, n_parts, n_rest).then_inc(s_nparts, 1)
                else:
                    dve.wait_ge(s_nsb, i + 2)
                    nc.vector.tensor_scalar(r_norm, n_sb, 1.0 / NORM_EPS, None, ALU.min).then_inc(s_rn, 1)
                    for ft in range(NQK):
                        dve.wait_ge(s_e, 4 * i + ft + 1)
                        nc.vector.tensor_tensor(proj[:, ft, :], m.psS[ft % 2][:, 512:1024], proj[:, ft, :], ALU.mult)\
                            .then_inc(s_efree, 1)
                        dve.wait_ge(s_efree, 4 * i + ft + 3)
                        split(ft)

            with dve.Fori(0, TB // 2) as ii:
                for par in range(2):
                    dve_block(2 * ii + par, projs[par])


def attention_phase(nc, m, io, L):
    pre = f"a{L}"
    UNITS = KT * B
    RING = 8
    ring = m.area(0, RING, T)
    q_ring = m.area(RING * T, 4, T)
    HALVES = (1, 0)
    LAG_PV = 5
    LAG_INV, LAG_SQ = 2, 3
    ACT_POW = 1656
    POW_STEPS = 10
    BATCH = 4
    ACT_SQ = 992
    rows = ROWS + NORM_ROWS if L == 0 else ROWS
    loads = 2 * len(PRODUCTS) + (2 if L == 0 else 0)
    values = m.values[:, :, :].rearrange("p (b k) (h d) -> p b k h d", b=B, h=HEADS)
    gated = m.gated[:, :, :].rearrange("p (b q a) (h d) -> p b q a h d", b=B, q=QB, h=HEADS)
    EPS_SUM = SHEP_EPS if L == 0 else SUM_EPS1
    with ExitStack() as ctx:
        (s_qk, s_pv, s_fin, s_h, s_r, s_yps, s_yo, s_yst, s_o, s_ot, s_den, s_rec, s_g, s_vt) = sems(
            nc, ctx, pre, "scores", "pv", "ffn_loaded", "ffn_hidden", "ffn_relu", "ffn_sum", "ffn_copied",
            "ffn_stored", "out_copied", "out_transposed", "den", "rec", "gated", "v_tile")
        if L == 0:
            s_a, s_y, s_m, s_v, s_wa, s_wd, s_r2, s_g0 = sems(
                nc, ctx, pre, "inv_dist", "quot", "guarded", "inv_shifted", "w_act", "w_dve", "ffn_squared", "gated0")
        else:
            s_cl, s_q, s_rs, s_ls, s_z, s_at, s_ln, s_w, s_pw = sems(
                nc, ctx, pre, "clipped", "cos2", "rsin", "log_sin", "tan_half", "angle", "log", "w_act", "w_dve")
        s_stk = sems(nc, ctx, pre, "stack0", "stack1")
        block = ctx.enter_context(nc.Block())

        def pairs(eng, body):
            body(0, True, False)
            with eng.Fori(1, HEADS - 1) as h:
                body(h, False, False)
            body(HEADS - 1, False, True)

        @block.sync
        def _(sp):
            def head(h, first, last):
                for b in range(B):
                    if not first:
                        sp.wait_ge(s_qk, 2 * (UNITS * h + KT * b + KT - UNITS))
                    tok = slice(b * T, (b + 1) * T)
                    for side, stack in ((0, m.q_stack[b]), (1, m.k_stack[b])):
                        for g, pr in enumerate(PRODUCTS):
                            sp.dma_start(stack[g * DH:(g + 1) * DH, :],
                                         io["qk_parts"][pr[side], bass.ds(h * DH + side * D, DH), tok])\
                                .then_inc(s_stk[b], 16)
                        if L == 0:
                            at = ROWS + 3 * side
                            sp.dma_start(stack[at:at + 3, :],
                                         io["norm_parts"][:, bass.ds(h + HEADS * side, 1), tok]
                                         .rearrange("a o t -> (a o) t")).then_inc(s_stk[b], 16)
                    if not (first and b == 0):
                        sp.wait_ge(s_h, 2 * (2 * h + b))
                    sp.dma_start(m.ffn_in[:, :, :], io["xT_store"][:, :, bass.ds((2 * h + b) * P, P)])\
                        .then_inc(s_fin, 16)
            pairs(sp, head)

        @block.gpsimd
        def _(pool):
            def head(h, first, last):
                for b in range(B):
                    if not first:
                        pool.wait_ge(s_pv, UNITS * h + KT * b + KT - UNITS)
                    nc.gpsimd.tensor_copy(m.v_tile[b][:, :, 0:DH], values[:, b, :, h, :]).then_inc(s_vt, 1)
            pairs(pool, head)

        def pe_scores(pe, h, u, first, halves=(0, 1)):
            b, kt = u // KT, u % KT
            if kt == 0 and halves[0] == 0:
                pe.wait_ge(s_stk[b], 16 * loads * (h + 1))
            for half in halves:
                if not (first and u == 0):
                    pe.wait_ge(s_y if L == 0 else s_cl, 2 * (UNITS * h + u) + half - 1)
                for q in range(2):
                    c = (2 * half + q) * 512
                    last = nc.tensor.matmul(m.psS[half][:, q * 512:(q + 1) * 512],
                                            m.k_stack[b][0:rows, kt * P:(kt + 1) * P],
                                            m.q_stack[b][0:rows, c:c + 512], start=True, stop=True)
                last.then_inc(s_qk, 1)

        def pe_values(pe, h, u, first):
            n = UNITS * h + u
            b, kt = (u % UNITS) // KT, u % KT
            if kt == 0:
                pe.wait_ge(s_vt, 2 * h + (u // KT) + 1)
                if not (first and 0 <= u < UNITS):
                    pe.wait_ge(s_o, 2 * h + (u // KT) - 1)
            if L == 0:
                pe.wait_ge(s_wa, n + 1)
                pe.wait_ge(s_wd, n + 1)
            else:
                pe.wait_ge(s_w, n + 1)
                pe.wait_ge(s_pw, POW_STEPS * (UNITS // BATCH * h + u // BATCH + 1))
            for q in range(QB):
                last = nc.tensor.matmul(m.psO[b][VW * q:VW * (q + 1), :], m.v_tile[b][:, kt, :],
                                        ring[:, u % RING, q * 512:(q + 1) * 512], start=kt == 0, stop=kt == KT - 1)
            last.then_inc(s_pv, 1)

        def pe_out(pe, n):
            pe.wait_ge(s_o, n + 1)
            for a in range(4):
                last = nc.tensor.transpose(m.psM[1][:, a * P:(a + 1) * P], m.head_outT[:, a * P:(a + 1) * P],
                                           m.ident[:, :])
            last.then_inc(s_ot, 1)

        def pe_hidden(pe, n, quarters=range(4)):
            for quarter in quarters:
                if quarter == 0:
                    pe.wait_ge(s_fin, 16 * (n + 1))
                g = HALVES[quarter // 2]
                for f in range(2 * (quarter % 2), 2 * (quarter % 2) + 2):
                    for k in range(KD):
                        c = (4 * g + f) * P
                        last = nc.tensor.matmul(m.psM[g][:, f * P:(f + 1) * P], m.w1T[:, k, c:c + P],
                                                m.ffn_in[:, k, :], start=k == 0 and (L == 0 or f == 0),
                                                stop=L == 0 and k == KD - 1)
                if quarter % 2 == 0:
                    continue
                if L == 1:
                    last = nc.tensor.matmul(m.psM[g][:, :], m.b1_tiles[:, :],
                                            m.ident[0:FT, 4 * g:4 * g + 4].unsqueeze(2).broadcast_to([FT, 4, P]),
                                            start=False, stop=True)
                last.then_inc(s_h, 1)

        def pe_ffn_sum(pe, n, fs=range(FT)):
            if fs[0] == 0:
                pe.wait_ge(s_r if L == 1 else s_r2, 2 * (n + 1))
            for f in fs:
                last = nc.tensor.matmul(m.psM[0][:, 0:D], m.hidden[:, f, :], m.w2T[:, f, :], start=f == 0,
                                        stop=L == 0 and f == FT - 1)
            if L == 1:
                last = nc.tensor.matmul(m.psM[0][:, 0:D], m.ones_row[0:1, :], m.b2_row[0:1, :], start=False, stop=True)
            if fs[-1] == FT - 1:
                last.then_inc(s_yps, 1)

        def act_out(act, n, b):
            act.wait_ge(s_pv, KT * (n + 1))
            act.wait_ge(s_ot, n)
            nc.scalar.activation(m.head_outT[:, :], m.psO[b][:, :], ACT.Copy).then_inc(s_o, 1)

        def act_relu(act, n, order=range(2)):
            act.wait_ge(s_yps, n)
            for i in order:
                g = HALVES[i]
                act.wait_ge(s_h, 2 * n + i + 1)
                nc.scalar.activation(m.hidden[:, 4 * g:4 * g + 4, :], m.psM[g][:, :].rearrange("p (f t) -> p f t", f=4),
                                     ACT.Relu).then_inc(s_r, 1)

        def act_ffn_out(act, n):
            act.wait_ge(s_yps, n + 1)
            act.wait_ge(s_yst, 16 * n)
            nc.scalar.activation(m.ffn_out[:, :], m.psM[0][:, 0:D], ACT.Copy).then_inc(s_yo, 1)
            act.wait_ge(s_yo, n + 1)
            act.dma_start(io["y_store"][bass.ds(n, 1), :, :].rearrange("o p d -> (o p) d"), m.ffn_out[:, :])\
                .then_inc(s_yst, 16)

        def dve_out(dve, h, b, n):
            dve.wait_ge(s_ot, n + 1)
            ps = m.psM[1][:, :].rearrange("p (a q c) -> p q a c", a=4, q=QB)
            den = m.den[:, 0, :].rearrange("p (q a) -> p q a", q=QB)
            rec = m.den[:, 1, :].rearrange("p (q a) -> p q a", q=QB)
            nc.vector.tensor_scalar(den, ps[:, :, :, DH], EPS_SUM, None, ALU.add).then_inc(s_den, 1)
            dve.wait_ge(s_den, n + 1)
            nc.vector.reciprocal(m.den[:, 1, :], m.den[:, 0, :]).then_inc(s_rec, 1)
            dve.wait_ge(s_rec, n + 1)
            out = gated[:, b, :, :, h, :]
            rec16 = rec.unsqueeze(3).broadcast_to([P, QB, 4, DH])
            if L == 0:
                nc.vector.tensor_tensor(out, ps[:, :, :, 0:DH], out, ALU.mult).then_inc(s_g0, 1)
                dve.wait_ge(s_g0, n + 1)
                nc.vector.tensor_tensor(out, out, rec16, ALU.mult).then_inc(s_g, 1)
            else:
                nc.vector.tensor_tensor(out, ps[:, :, :, 0:DH], rec16, ALU.mult).then_inc(s_g, 1)

        if L == 0:
            OUT_COPY, OUT_T, OUT_DIV = 5, 7, 8
            HID = (0, 1, 2, 3)
            RELU, SQ = (2, 4), (4, 6)
            SUM = {8: (0,), 9: (1,), 10: (2,), 11: (3,), 12: (4,), 13: (5,), 14: (6, 7)}
            COPY = 15

            @block.tensor
            def _(pe):
                def head(h, first, last):
                    for u in range(UNITS + (LAG_PV if last else 0)):
                        b, kt = u // KT, u % KT
                        n = 2 * h + b
                        if u < UNITS:
                            pe_scores(pe, h, u, first, (0,))
                        if not (first and u < LAG_PV):
                            pe_values(pe, h, u - LAG_PV, first)
                        if u < UNITS:
                            pe_scores(pe, h, u, first, (1,))
                        if kt == 0 and not first:
                            pe.wait_ge(s_g, n - 1)
                        if kt == 2 and not (first and b == 0):
                            pe.wait_ge(s_yo, n)
                        if kt in HID and u < UNITS:
                            pe_hidden(pe, n, (HID.index(kt),))
                        if kt == OUT_T and u < UNITS and not (first and b == 0):
                            pe.wait_ge(s_r, 2 * n + 1)
                            pe_out(pe, n - 1)
                        if kt in SUM:
                            pe_ffn_sum(pe, n, SUM[kt])
                    if last:
                        pe_out(pe, 2 * HEADS - 1)
                pairs(pe, head)

            @block.scalar
            def _(act):
                def head(h, first, last):
                    def inverse_distance(u, half):
                        c = UNITS * h + u
                        if half == 0 and not (first and u < RING):
                            act.wait_ge(s_pv, c - RING + 1)
                        act.wait_ge(s_qk, 2 * c + half + 1)
                        nc.scalar.activation(ring[:, u % RING, half * 1024:(half + 1) * 1024],
                                             m.psS[half][:, :], ACT.Abs_reciprocal_sqrt, bias=ZERO_SHIFT)\
                            .then_inc(s_a, 1)

                    for u in range(UNITS + (LAG_SQ if last else 0)):
                        b, kt = u // KT, u % KT
                        n = 2 * h + b
                        c = UNITS * h + u
                        if u < UNITS:
                            inverse_distance(u, 0)
                        if u < UNITS + LAG_INV and not (first and u < LAG_INV):
                            act.wait_ge(s_m, c - LAG_INV + 1)
                            slot = ring[:, (u - LAG_INV) % RING, :]
                            nc.scalar.activation(slot, slot, ACT.Abs_reciprocal_sqrt, bias=SHEP_EPS * SHEP_EPS,
                                                 scale=2 * SHEP_EPS).then_inc(s_v, 1)
                        if u < UNITS:
                            inverse_distance(u, 1)
                        if not (first and u < LAG_SQ):
                            act.wait_ge(s_v, c - LAG_SQ + 1)
                            slot = ring[:, (u - LAG_SQ) % RING, 0:ACT_SQ]
                            nc.scalar.activation(slot, slot, ACT.Square).then_inc(s_wa, 1)
                        if kt == OUT_COPY and not (first and b == 0) and u < UNITS:
                            act_out(act, n - 1, (b + 1) % 2)
                        if kt in RELU and u < UNITS:
                            act_relu(act, n, (RELU.index(kt),))
                        if kt == COPY:
                            act_ffn_out(act, n)
                    if last:
                        act_out(act, 2 * HEADS - 1, 1)
                        act.wait_ge(s_yst, 16 * 2 * HEADS)
                pairs(act, head)

            @block.vector
            def _(dve):
                def head(h, first, last):
                    def quotient(u, half):
                        c = UNITS * h + u
                        dve.wait_ge(s_a, 2 * c + half + 1)
                        part = ring[:, u % RING, half * 1024:(half + 1) * 1024]
                        nc.vector.scalar_tensor_tensor(part, part, 0.5 / SHEP_EPS, m.psS[half][:, :],
                                                       ALU.add, ALU.mult).then_inc(s_y, 1)

                    for u in range(UNITS + (LAG_SQ if last else 0)):
                        b, kt = u // KT, u % KT
                        n = 2 * h + b
                        c = UNITS * h + u
                        if u < UNITS:
                            quotient(u, 0)
                        if u <= UNITS and not (first and u < 1):
                            dve.wait_ge(s_y, 2 * c)
                            slot = ring[:, (u - 1) % RING, :]
                            nc.vector.tensor_scalar(slot, slot, 0.0, None, ALU.max).then_inc(s_m, 1)
                        if u < UNITS:
                            quotient(u, 1)
                        if not (first and u < LAG_SQ):
                            dve.wait_ge(s_v, c - LAG_SQ + 1)
                            part = ring[:, (u - LAG_SQ) % RING, ACT_SQ:T]
                            nc.vector.tensor_tensor(part, part, part, ALU.mult).then_inc(s_wd, 1)
                        if kt == OUT_DIV and not (first and b == 0) and u < UNITS:
                            dve_out(dve, h if b else h - 1, 1 - b, n - 1)
                        if kt in SQ:
                            g = HALVES[SQ.index(kt)]
                            dve.wait_ge(s_r, 2 * n + SQ.index(kt) + 1)
                            part = m.hidden[:, 4 * g:4 * g + 4, :]
                            nc.vector.tensor_tensor(part, part, part, ALU.mult).then_inc(s_r2, 1)
                    if last:
                        dve_out(dve, HEADS - 1, 1, 2 * HEADS - 1)
                pairs(dve, head)
        else:
            NB = UNITS // BATCH

            @block.tensor
            def _(pe):
                def head(h, first, last):
                    for j in range(NB + (1 if last else 0)):
                        n = 2 * h + j // 4
                        if first and j == 0:
                            pe_scores(pe, h, 0, True)
                        for u in range(BATCH * j + 1, min(BATCH * (j + 1) + 1, UNITS)):
                            pe_scores(pe, h, u, first)
                        if j == NB - 1 and not last:
                            pe_scores(pe, h + 1, 0, False)
                        if not (first and j == 0):
                            for u in range(BATCH * (j - 1), BATCH * j):
                                pe_values(pe, h, u, first)
                        if j % 4 == 1 and not (first and j < 4):
                            pe_out(pe, n - 1)
                        if j % 4 == 2:
                            if not (first and j < 4):
                                pe.wait_ge(s_yo, n)
                                pe.wait_ge(s_g, n)
                            pe_hidden(pe, n)
                        if j % 4 == 3:
                            pe_ffn_sum(pe, n)
                    if last:
                        pe_out(pe, 2 * HEADS - 1)
                pairs(pe, head)

            @block.scalar
            def _(act):
                def head(h, first, last):
                    for j in range(NB):
                        n = 2 * h + j // 4
                        twos = [(BATCH * j + 2 * i, BATCH * j + 2 * i + 1) for i in range(BATCH // 2)]
                        if j == 0:
                            nc.scalar.preload_act_table_set("natural_log_exp_and_others")
                        for u, v in twos:
                            act.wait_ge(s_q, UNITS * h + v + 1)
                            pair = q_ring[:, u % BATCH:u % BATCH + 2, :]
                            nc.scalar.activation(pair, pair, ACT.Ln, bias=1.0, scale=-1.0).then_inc(s_ls, 1)
                        for u in range(BATCH * j, BATCH * (j + 1)):
                            act.wait_ge(s_ls, UNITS // 2 * h + u // 2 + 1)
                            slot = q_ring[:, u % BATCH, :]
                            nc.scalar.activation(slot, slot, ACT.Sigmoid, scale=-0.5).then_inc(s_rs, 1)
                        for u, v in twos:
                            act.wait_ge(s_z, UNITS * h + v + 1)
                            pair = ring[:, u % RING:u % RING + 2, :]
                            nc.scalar.activation(pair, pair, ACT.Arctan).then_inc(s_at, 1)
                        nc.scalar.preload_act_table_set("natural_log_exp_and_others")
                        for u, v in twos:
                            act.wait_ge(s_at, UNITS // 2 * h + u // 2 + 1)
                            pair = ring[:, u % RING:u % RING + 2, 0:ACT_POW]
                            nc.scalar.activation(pair, pair, ACT.Ln, bias=0.5, scale=2.0 / PI)\
                                .then_inc(s_ln, 1)
                        for u, v in twos:
                            act.wait_ge(s_ln, UNITS // 2 * h + u // 2 + 1)
                            pair = ring[:, u % RING:u % RING + 2, 0:ACT_POW]
                            nc.scalar.activation(pair, pair, ACT.Exp, scale=16.0).then_inc(s_w, 2)
                        if j % 4 == 0 and not (first and j == 0):
                            act_out(act, n - 1, (j // 4 + 1) % 2)
                        if j % 4 == 2:
                            act_relu(act, n)
                        if j % 4 == 3:
                            act_ffn_out(act, n)
                    if last:
                        act_out(act, 2 * HEADS - 1, 1)
                        act.wait_ge(s_yst, 16 * 2 * HEADS)
                pairs(act, head)

            @block.vector
            def _(dve):
                def head(h, first, last):
                    def cosines(u):
                        c = UNITS * h + u
                        if not (first and u < RING):
                            dve.wait_ge(s_pv, c - RING + 1)
                        for half in range(2):
                            dve.wait_ge(s_qk, 2 * c + half + 1)
                            nc.vector.tensor_scalar(ring[:, u % RING, half * 1024:(half + 1) * 1024],
                                                    m.psS[half][:, :], COS_MAX, -COS_MAX, ALU.min, ALU.max)\
                                .then_inc(s_cl, 1)

                    def square_cosines(u):
                        c = UNITS * h + u
                        dve.wait_ge(s_cl, 2 * c + 2)
                        nc.vector.tensor_tensor(q_ring[:, u % BATCH, :], ring[:, u % RING, :], ring[:, u % RING, :],
                                                ALU.mult).then_inc(s_q, 1)

                    def powers(j):
                        dve.wait_ge(s_at, UNITS // 2 * h + 2 * j + 2)
                        first_slot = (BATCH * j) % RING
                        parts = [ring[:, at:at + BATCH // 2, ACT_POW:T] for at in (first_slot, first_slot + BATCH // 2)]
                        done = POW_STEPS * (NB * h + j)
                        for part in parts:
                            nc.vector.tensor_scalar(part, part, 2.0 / PI, 0.5, ALU.mult, ALU.add).then_inc(s_pw, 1)
                        for i in range(2, POW_STEPS):
                            part = parts[i % 2]
                            dve.wait_ge(s_pw, done + i - 1)
                            nc.vector.tensor_tensor(part, part, part, ALU.mult).then_inc(s_pw, 1)

                    for j in range(NB + (1 if last else 0)):
                        n = 2 * h + j // 4
                        us = range(BATCH * j, BATCH * (j + 1))
                        if j < NB:
                            cosines(us[0])
                            cosines(us[1])
                            square_cosines(us[0])
                            square_cosines(us[1])
                            cosines(us[2])
                            cosines(us[3])
                            square_cosines(us[2])
                            square_cosines(us[3])
                        if not (first and j == 0):
                            powers(j - 1)
                        if j < NB:
                            for u in us:
                                dve.wait_ge(s_rs, UNITS * h + u + 1)
                                slot = ring[:, u % RING, :]
                                nc.vector.tensor_tensor(slot, slot, q_ring[:, u % BATCH, :], ALU.mult).then_inc(s_z, 1)
                            dve.wait_ge(s_z, UNITS * h + BATCH * (j + 1))
                        if j < NB and j % 4 == 1 and not (first and j < 4):
                            dve_out(dve, h if j >= 4 else h - 1, (j // 4 + 1) % 2, n - 1)
                    if last:
                        dve_out(dve, HEADS - 1, 1, 2 * HEADS - 1)
                pairs(dve, head)


def output_phase(nc, m, io, L):
    pre = f"o{L}"
    x_sb = m.area(0, NT, D)
    xn_sb = m.area(NT * D, NT, D)
    g_sb = m.area(2 * NT * D, NT, D)
    woT = m.hidden[:, 0:4, :].rearrange("p (k a) b -> p k (a b)", k=KD)
    bo = m.ffn_out[0:1, :]
    oT = [m.w1T[:, i, 0:2 * D].rearrange("p (a k t) -> p a k t", a=2, k=KD) for i in range(2)]
    tmp = [m.w2T[:, 2 * i:2 * i + 2, :] for i in range(2)]
    CH = 4
    PAIRS = NT // 2
    CP = PAIRS // CH
    with ExitStack() as ctx:
        s_w, s_silu, s_tr, s_oT, s_mm, s_free, s_sg, s_x, s_st = sems(
            nc, ctx, pre, "weights", "silu", "transposed", "copied", "product", "free", "sg", "x", "stored")
        s_load = sems(nc, ctx, pre, *[f"load{c}" for c in range(CH)])
        (s_next,) = sems(nc, ctx, pre, "next_weights")
        block = ctx.enter_context(nc.Block())
        n_loads = 3 if L == 0 else 2
        x_view = (io["x"] if L == 0 else io["x1_store"]).rearrange("(t p) d -> p t d", p=P)
        out_view = (io["x1_store"] if L == 0 else io["out"]).rearrange("(t p) d -> p t d", p=P)

        def pair(buf, n):
            return buf[:, bass.ds(2 * n, 2), :]

        @block.sync
        def _(sp):
            sp.dma_start(woT, io["woT"].rearrange("(k p) n -> p k n", p=P)).then_inc(s_w, 16)
            sp.dma_start(bo, io["bo"]).then_inc(s_w, 16)
            for c in range(CH):
                t = slice(2 * CP * c, 2 * CP * (c + 1))
                sp.dma_start(g_sb[:, t, :], io["y_store"].rearrange("t p d -> p t d")[:, t, :]).then_inc(s_load[c], 16)
                if L == 0:
                    sp.dma_start(xn_sb[:, t, :], io["xn_store"][:, t, :]).then_inc(s_load[c], 16)
                sp.dma_start(x_sb[:, t, :], x_view[:, t, :]).then_inc(s_load[c], 16)
            next_loads = load_weights(sp, m, io, 1, s_next) if L == 0 else 0
            for c in range(CH):
                t = slice(2 * CP * c, 2 * CP * (c + 1))
                sp.wait_ge(s_x, CP * (c + 1))
                sp.dma_start(out_view[:, t, :], x_sb[:, t, :]).then_inc(s_st, 16)
            sp.wait_ge(s_st, 16 * CH)
            if L == 0:
                sp.wait_ge(s_next, next_loads)

        @block.tensor
        def _(pe):
            def transposes(n):
                if n >= 2:
                    pe.wait_ge(s_oT, n - 1)
                for a in range(2):
                    for k in range(KD):
                        c = (KD * a + k) * P
                        last = nc.tensor.transpose(m.psS[n % 2][:, c:c + P], m.gated[:, 2 * n + a, k * P:(k + 1) * P],
                                                   m.ident[:, :])
                last.then_inc(s_tr, 1)

            transposes(0)
            pe.wait_ge(s_w, 32)
            for n in range(PAIRS):
                if n + 1 < PAIRS:
                    transposes(n + 1)
                if n >= 2:
                    pe.wait_ge(s_free, n - 1)
                nc.tensor.matmul(m.psO[n % 2][:, :], m.ones_row[0:1, :], bo.unsqueeze(1).broadcast_to([1, 2, D]),
                                 start=True, stop=False)
                pe.wait_ge(s_oT, n + 1)
                for a in range(2):
                    for k in range(KD):
                        last = nc.tensor.matmul(m.psO[n % 2][:, a * D:(a + 1) * D], oT[n % 2][:, a, k, :],
                                                woT[:, k, :], start=False, stop=a == 1 and k == KD - 1)
                last.then_inc(s_mm, 1)

        @block.scalar
        def _(act):
            act.sem_inc(s_mm, 1)
            for c in range(CH):
                act.wait_ge(s_load[c], 16 * n_loads)
                g = g_sb[:, 2 * CP * c:2 * CP * (c + 1), :]
                nc.scalar.activation(g, g, ACT.Silu).then_inc(s_silu, 1)
                with act.Fori(0, CP // 2) as i:
                    for par in range(2):
                        n = CP * c + 2 * i + par
                        act.wait_ge(s_tr, n + 1)
                        act.wait_ge(s_mm, n + 1)
                        nc.scalar.activation(oT[par], m.psS[par][:, 0:2 * D]
                                             .rearrange("p (a k t) -> p a k t", a=2, k=KD), ACT.Copy).then_inc(s_oT, 1)

        @block.vector
        def _(dve):
            for c in range(CH):
                dve.wait_ge(s_silu, c + 1)
                dve.wait_ge(s_load[c], 16 * n_loads)
                with dve.Fori(0, CP // 2) as i:
                    for par in range(2):
                        n = CP * c + 2 * i + par
                        dve.wait_ge(s_mm, n + 2)
                        ps = m.psO[par][:, :].rearrange("p (a d) -> p a d", a=2)
                        if L == 0:
                            nc.vector.tensor_tensor(tmp[par], ps, pair(xn_sb, n), ALU.add).then_inc(s_free, 1)
                            dve.wait_ge(s_free, n + 1)
                            nc.vector.tensor_tensor(tmp[par], tmp[par], pair(g_sb, n), ALU.mult).then_inc(s_sg, 1)
                            dve.wait_ge(s_sg, n + 1)
                        else:
                            nc.vector.tensor_tensor(tmp[par], ps, pair(g_sb, n), ALU.mult).then_inc(s_free, 1)
                            dve.wait_ge(s_free, n + 1)
                        nc.vector.tensor_tensor(pair(x_sb, n), pair(x_sb, n), tmp[par], ALU.add).then_inc(s_x, 1)


def program(nc, ins, out):
    with ExitStack() as ctx:
        m = Mem(nc, ctx)
        scratch = {
            "qk_parts": ((3, 2 * D, B * T), BF16), "norm_parts": ((3, 2 * HEADS, B * T), BF16),
            "xn_store": ((P, NT, D), F32), "xT_store": ((P, KD, B * T), F32), "y_store": ((NT, P, D), F32),
            "x1_store": ((B * T, D), F32),
        }
        io = dict(ins)
        io["out"] = out
        for name, (shape, dt) in scratch.items():
            io[name] = nc.dram_tensor(name, shape, dt, kind="Internal").ap()
        constants_phase(nc, m, io)
        for L in range(2):
            mine = dict(io)
            for name in ("wqk", "wvg", "woT", "bo"):
                mine[name] = io[f"{name}{L}"]
            weights_phase(nc, m, mine, L)
            norm_phase(nc, m, mine, L)
            projection_phase(nc, m, mine, L)
            attention_phase(nc, m, mine, L)
            output_phase(nc, m, mine, L)


def layout(inputs):
    import numpy as np

    a = {k: np.asarray(v) for k, v in inputs.items()}
    w_in = a["L0_attn_W_in"].reshape(HEADS, 4, DH, D)
    b_in = a["L0_attn_b_in"].reshape(HEADS, 4, DH)
    q, k, v, g = (w_in[:, i].reshape(D, D).T for i in range(4))
    bq, bk, bv, bg = (b_in[:, i].reshape(D) for i in range(4))
    sel = np.zeros((P, NCOL), np.float32)
    sel[np.arange(P), np.arange(P) // DH] = 1.0
    arrays = {
        "x": a["L0_attn_X"].reshape(B * T, D),
        "wqk0": np.concatenate([q, k], axis=1), "wvg0": np.concatenate([v, g], axis=1),
        "bqk": np.concatenate([bq, bk]).reshape(NQK, P).T, "bvg": np.concatenate([bv, bg]).reshape(1, 2 * D),
        "woT0": a["L0_attn_W_out"].T, "bo0": a["L0_attn_b_out"].reshape(1, D),
        "fast_bT": a["L0_ffn_fast_b"].T, "w_fc": a["L0_ffn_w_fc"], "w_proj": a["L0_ffn_w_proj"],
        "u_T": a["L0_ffn_u"].T, "v": a["L0_ffn_v"], "gate": a["L0_ffn_gate"].reshape(1, 1),
        "wqk1": np.concatenate([a["L1_attn_Wq"].T, a["L1_attn_Wk"].T], axis=1), "wvg1": a["L1_attn_Wv"].T,
        "woT1": a["L1_attn_Wo"].T, "bo1": a["L1_attn_bo"].reshape(1, D),
        "W1": a["L1_ffn_W1"], "b1": a["L1_ffn_b1"].reshape(FT, P), "W2": a["L1_ffn_W2"],
        "b2": a["L1_ffn_b2"].reshape(1, D),
        "ident": np.eye(P, dtype=np.float32), "sel": sel, "selT": np.tile(sel.T, (NQK, 1)),
    }
    return {k: np.ascontiguousarray(v) for k, v in arrays.items()}


def kernel(**inputs):
    import concourse.bacc as bacc
    from concourse.bass_utils import run_bass_kernel_spmd

    nc = bacc.Bacc("TRN2", target_bir_lowering=False, num_devices=1)
    arrays = layout(inputs)
    ins = {k: nc.dram_tensor(f"in_{k}", v.shape, mybir.dt.from_np(v.dtype), kind="ExternalInput").ap()
           for k, v in arrays.items()}
    out = nc.dram_tensor("out", (B * T, D), F32, kind="ExternalOutput").ap()
    program(nc, ins, out)
    r = run_bass_kernel_spmd(nc, [{f"in_{k}": v for k, v in arrays.items()}], core_ids=[0])
    return r.results[0]["out"].reshape(B, T, D)
```
